# Optimizing a Trainium2 kernel written in Bass

```python
import numpy as np
import jax
import jax.numpy as jnp

def _softmax(x, axis=-1):
    return jax.nn.softmax(x, axis=axis)

def _gelu(x):
    return jax.nn.gelu(x, approximate=True)

def _silu(x):
    return jax.nn.silu(x)

def _sigmoid(x):
    return jax.nn.sigmoid(x)

def _layernorm(x, axis=-1, eps=1e-05):
    m = jnp.mean(x, axis=axis, keepdims=True)
    v = jnp.var(x, axis=axis, keepdims=True)
    return (x - m) / jnp.sqrt(v + eps)

def _scatter_add(tgt, idx, src, axis=0):
    return tgt.at[idx].add(src)

def _segment_sum(src, seg, n):
    return jax.ops.segment_sum(src, seg, n)
kernel_name = 'mk_xattn_ffn_d2_seqx_r4_9ff374'

def setup_inputs(seed: int=0):
    np.random.seed(seed)
    _w = jnp.asarray

    def _rec_inputs():
        import jax
        import jax.numpy as jnp
        _rk = jax.random.key(seed)
        x = -0.000125 + 0.9999 * jax.random.normal(jax.random.fold_in(_rk, 1), (2, 512, 1024), jnp.float32)
        _lenS = 512 - jax.random.randint(jax.random.fold_in(_rk, 7), (2,), 0, max(1, 512 // 4) + 1, jnp.int32)
        _lenS2 = 1024 - jax.random.randint(jax.random.fold_in(_rk, 8), (2,), 0, max(1, 1024 // 4) + 1, jnp.int32)
        _ctx_4096P = jax.random.normal(jax.random.fold_in(_rk, 11), (2, 16, 1024), jnp.float32)
        _ctx_4096c = jax.random.dirichlet(jax.random.fold_in(_rk, 511), 0.3 * jnp.ones((16,), jnp.float32), (2, 1024))
        _ctx_4096t = jnp.einsum('bsk,bkd->bsd', _ctx_4096c, _ctx_4096P)
        _ctx_4096t = _ctx_4096t * jax.lax.rsqrt(jnp.mean(jnp.square(_ctx_4096t)) + 1e-12) * 0.953939
        ctx_4096 = -5.72187e-05 + 0.999849 * (_ctx_4096t + 0.3 * jax.random.normal(jax.random.fold_in(_rk, 611), (2, 1024, 1024), jnp.float32))
        _validS = jnp.arange(512)[None, :] < _lenS[:, None]
        _validS2 = jnp.arange(1024)[None, :] < _lenS2[:, None]
        _causal = jnp.tril(jnp.ones((512, 512), dtype=bool))
        mask_BxSxS2_ff0 = jnp.where(jnp.ones((2, 512, 1024), dtype=bool), 0.0, -1000000000.0).astype(jnp.float32)
        return (x, ctx_4096, mask_BxSxS2_ff0)
    x, ctx_4096, mask_BxSxS2_ff0 = _rec_inputs()

    def _L0_xattn_setup():
        import jax, jax.numpy as jnp
        import numpy as np
        QMIN = 0.0
        QMAX = 255.0

        def fake_quant(x, scale, zp):
            s = scale.reshape(())
            z = zp.reshape(())
            q = jnp.clip(jnp.round(x / s + z), QMIN, QMAX)
            return (q - z) * s
        key = jax.random.key(seed)
        k1, k2 = jax.random.split(key)
        B, M, K, N = (4, 512, 1024, 1024)
        x1 = jax.random.normal(k1, (B, M, K), dtype=jnp.float32)
        x2 = jax.random.normal(k2, (B, K, N), dtype=jnp.float32)
        x1_scale = jnp.full((1,), 8.0 / 255.0, dtype=jnp.float32)
        x1_zp = jnp.full((1,), 128.0, dtype=jnp.float32)
        x2_scale = jnp.full((1,), 8.0 / 255.0, dtype=jnp.float32)
        x2_zp = jnp.full((1,), 128.0, dtype=jnp.float32)
        return {'x1': x1, 'x2': x2, 'x1_scale': x1_scale, 'x1_zp': x1_zp, 'x2_scale': x2_scale, 'x2_zp': x2_zp}
    _L0_xattn_all = _L0_xattn_setup()
    _L0_xattn_in = {k: v for k, v in _L0_xattn_all.items() if k in ('x1_scale', 'x1_zp', 'x2_scale', 'x2_zp')}
    del _L0_xattn_all

    def _L0_ffn_setup():
        import jax, jax.numpy as jnp
        import numpy as np
        IMAGE_START_POS = 34
        Q_START = IMAGE_START_POS + 144 + 1
        Q_END = -1
        LORA_ALPHA = 32
        LORA_RANK = 16
        SCALING = LORA_ALPHA / LORA_RANK
        key = jax.random.key(seed)
        ks = jax.random.split(key, 7)
        B_, S, D, O, E, R = (4, 512, 1024, 1024, 8, LORA_RANK)
        s = 0.02
        return {'x': jax.random.normal(ks[0], (B_, S, D), jnp.float32), 'W': jax.random.normal(ks[1], (O, D), jnp.float32) * s, 'b': jax.random.normal(ks[2], (O,), jnp.float32) * s, 'A': jax.random.normal(ks[3], (E, R, D), jnp.float32) * s, 'B': jax.random.normal(ks[4], (E, O, R), jnp.float32) * s, 'router_W': jax.random.normal(ks[5], (E, D), jnp.float32) * s, 'router_b': jax.random.normal(ks[6], (E,), jnp.float32) * s}
    _L0_ffn_all = _L0_ffn_setup()
    _L0_ffn_in = {k: v for k, v in _L0_ffn_all.items() if k in ('W', 'b', 'A', 'B', 'router_W', 'router_b')}
    del _L0_ffn_all

    def _L1_xattn_setup():
        import jax, jax.numpy as jnp
        import numpy as np
        BS, SEQ, D_MODEL = (4, 256, 1024)
        N_Q_HEADS, N_KV_HEADS, D_K, D_V = (32, 8, 128, 128)
        ROPE_BASE = 10000.0

        def _rotate_half(x):
            x1, x2 = jnp.split(x, 2, axis=-1)
            return jnp.concatenate([-x2, x1], axis=-1)

        def _apply_rope(x, pos0):
            d = x.shape[-1]
            seq = x.shape[2]
            inv_freq = 1.0 / ROPE_BASE ** (jnp.arange(0, d, 2, dtype=jnp.float32) / d)
            pos = (pos0 + jnp.arange(seq)).astype(jnp.float32)
            ang = pos[:, None] * inv_freq[None, :]
            cos = jnp.concatenate([jnp.cos(ang), jnp.cos(ang)], axis=-1)
            sin = jnp.concatenate([jnp.sin(ang), jnp.sin(ang)], axis=-1)
            return x * cos[None, None] + _rotate_half(x) * sin[None, None]
        key = jax.random.key(seed)
        ks = jax.random.split(key, 8)
        w_scale = 0.02
        return {'query': jax.random.normal(ks[0], (BS, SEQ, D_MODEL), dtype=jnp.float32), 'key': jax.random.normal(ks[1], (BS, SEQ, D_MODEL), dtype=jnp.float32), 'value': jax.random.normal(ks[2], (BS, SEQ, D_MODEL), dtype=jnp.float32), 'mask': jnp.zeros((BS, SEQ, SEQ), dtype=jnp.float32), 'wq': jax.random.normal(ks[3], (D_MODEL, N_Q_HEADS * D_K), dtype=jnp.float32) * w_scale, 'wk': jax.random.normal(ks[4], (D_MODEL, N_KV_HEADS * D_K), dtype=jnp.float32) * w_scale, 'wv': jax.random.normal(ks[5], (D_MODEL, N_KV_HEADS * D_V), dtype=jnp.float32) * w_scale, 'wo': jax.random.normal(ks[6], (N_Q_HEADS * D_V, D_MODEL), dtype=jnp.float32) * w_scale, 'curr_seq_pos': 0}
    _L1_xattn_all = _L1_xattn_setup()
    _L1_xattn_in = {k: v for k, v in _L1_xattn_all.items() if k in ('wq', 'wk', 'wv', 'wo')}
    del _L1_xattn_all

    def _L1_ffn_setup():
        import jax, jax.numpy as jnp
        import numpy as np
        NUM_EXPERTS = 4
        HIDDEN = 1024
        RANK = 8
        ALPHA = 8.0
        SCALE = ALPHA / RANK
        key = jax.random.key(seed)
        ks = jax.random.split(key, 6)
        B, T, H, E, R = (4, 1024, HIDDEN, NUM_EXPERTS, RANK)
        x = jax.random.normal(ks[0], (B, T, H), dtype=jnp.float32)
        W_up = jax.random.normal(ks[1], (H, H), dtype=jnp.float32) / np.sqrt(H)
        gate_w = jax.random.normal(ks[2], (E, H), dtype=jnp.float32) / np.sqrt(H)
        expert_bias = jnp.zeros((E,), dtype=jnp.float32)
        lora_A = jax.random.normal(ks[3], (E, R, H), dtype=jnp.float32) / np.sqrt(H)
        lora_B = jax.random.normal(ks[4], (E, H, R), dtype=jnp.float32) * 0.01
        return {'x': x, 'W_up': W_up, 'gate_w': gate_w, 'expert_bias': expert_bias, 'lora_A': lora_A, 'lora_B': lora_B}
    _L1_ffn_all = _L1_ffn_setup()
    _L1_ffn_in = {k: v for k, v in _L1_ffn_all.items() if k in ('W_up', 'gate_w', 'expert_bias', 'lora_A', 'lora_B')}
    del _L1_ffn_all
    return {'x': x, 'ctx_4096': ctx_4096, 'mask_BxSxS2_ff0': mask_BxSxS2_ff0, 'L0_xattn_x1_scale': _L0_xattn_in['x1_scale'], 'L0_xattn_x1_zp': _L0_xattn_in['x1_zp'], 'L0_xattn_x2_scale': _L0_xattn_in['x2_scale'], 'L0_xattn_x2_zp': _L0_xattn_in['x2_zp'], 'L0_ffn_W': _L0_ffn_in['W'], 'L0_ffn_b': _L0_ffn_in['b'], 'L0_ffn_A': _L0_ffn_in['A'], 'L0_ffn_B': _L0_ffn_in['B'], 'L0_ffn_router_W': _L0_ffn_in['router_W'], 'L0_ffn_router_b': _L0_ffn_in['router_b'], 'L1_xattn_wq': _L1_xattn_in['wq'], 'L1_xattn_wk': _L1_xattn_in['wk'], 'L1_xattn_wv': _L1_xattn_in['wv'], 'L1_xattn_wo': _L1_xattn_in['wo'], 'L1_ffn_W_up': _L1_ffn_in['W_up'], 'L1_ffn_gate_w': _L1_ffn_in['gate_w'], 'L1_ffn_expert_bias': _L1_ffn_in['expert_bias'], 'L1_ffn_lora_A': _L1_ffn_in['lora_A'], 'L1_ffn_lora_B': _L1_ffn_in['lora_B']}

def reference(x, ctx_4096, mask_BxSxS2_ff0, L0_xattn_x1_scale, L0_xattn_x1_zp, L0_xattn_x2_scale, L0_xattn_x2_zp, L0_ffn_W, L0_ffn_b, L0_ffn_A, L0_ffn_B, L0_ffn_router_W, L0_ffn_router_b, L1_xattn_wq, L1_xattn_wk, L1_xattn_wv, L1_xattn_wo, L1_ffn_W_up, L1_ffn_gate_w, L1_ffn_expert_bias, L1_ffn_lora_A, L1_ffn_lora_B):
    import jax
    import jax.numpy as jnp

    def _L0_xattn_ref(x1, x2, x1_scale, x1_zp, x2_scale, x2_zp):
        import jax, jax.numpy as jnp
        import numpy as np
        QMIN = 0.0
        QMAX = 255.0

        def fake_quant(x, scale, zp):
            s = scale.reshape(())
            z = zp.reshape(())
            q = jnp.clip(jnp.round(x / s + z), QMIN, QMAX)
            return (q - z) * s
        q1 = fake_quant(x1, x1_scale, x1_zp)
        q2 = fake_quant(x2, x2_scale, x2_zp)
        return jnp.matmul(q1, q2)

    def _L0_ffn_ref(x, W, b, A, B, router_W, router_b):
        import jax, jax.numpy as jnp
        import numpy as np
        IMAGE_START_POS = 34
        Q_START = IMAGE_START_POS + 144 + 1
        Q_END = -1
        LORA_ALPHA = 32
        LORA_RANK = 16
        SCALING = LORA_ALPHA / LORA_RANK
        x_q = x[:, Q_START:Q_END, :]
        q = x_q.mean(axis=1)
        logits = q @ router_W.T + router_b
        routing = jax.nn.softmax(logits, axis=-1)
        base = x @ W.T + b
        t = jnp.einsum('bsd,erd->bser', x, A)
        lora = jnp.einsum('bser,eor,be->bso', t, B, routing) * SCALING
        return base + lora

    def _L1_xattn_ref(query, key, value, mask, wq, wk, wv, wo, curr_seq_pos):
        import jax, jax.numpy as jnp
        import numpy as np
        BS, SEQ, D_MODEL = (4, 256, 1024)
        N_Q_HEADS, N_KV_HEADS, D_K, D_V = (32, 8, 128, 128)
        ROPE_BASE = 10000.0

        def _rotate_half(x):
            x1, x2 = jnp.split(x, 2, axis=-1)
            return jnp.concatenate([-x2, x1], axis=-1)

        def _apply_rope(x, pos0):
            d = x.shape[-1]
            seq = x.shape[2]
            inv_freq = 1.0 / ROPE_BASE ** (jnp.arange(0, d, 2, dtype=jnp.float32) / d)
            pos = (pos0 + jnp.arange(seq)).astype(jnp.float32)
            ang = pos[:, None] * inv_freq[None, :]
            cos = jnp.concatenate([jnp.cos(ang), jnp.cos(ang)], axis=-1)
            sin = jnp.concatenate([jnp.sin(ang), jnp.sin(ang)], axis=-1)
            return x * cos[None, None] + _rotate_half(x) * sin[None, None]
        bs, sq, _ = query.shape
        n_groups = N_Q_HEADS // N_KV_HEADS
        q = (query @ wq).reshape(bs, sq, N_Q_HEADS, D_K).transpose((0, 2, 1, 3))
        sk = key.shape[1]
        k = (key @ wk).reshape(bs, sk, N_KV_HEADS, 1, D_K)
        k = jnp.repeat(k, n_groups, axis=3).reshape(bs, sk, N_Q_HEADS, D_K).transpose((0, 2, 1, 3))
        v = (value @ wv).reshape(bs, sk, N_KV_HEADS, 1, D_V)
        v = jnp.repeat(v, n_groups, axis=3).reshape(bs, sk, N_Q_HEADS, D_V).transpose((0, 2, 1, 3))
        scale = jnp.sqrt(jnp.float32(D_K))
        q = _apply_rope(q, curr_seq_pos)
        k = _apply_rope(k, curr_seq_pos)
        raw = jnp.einsum('bhqd,bhkd->bhqk', q, k) / scale
        masked = raw + mask[:bs, None, curr_seq_pos:curr_seq_pos + sq, :sk]
        attn = jax.nn.softmax(masked, axis=-1)
        out = jnp.einsum('bhqk,bhkd->bhqd', attn, v)
        out = out.transpose((0, 2, 1, 3)).reshape(bs, sq, N_Q_HEADS * D_V)
        return out @ wo

    def _L1_ffn_ref(x, W_up, gate_w, expert_bias, lora_A, lora_B):
        import jax, jax.numpy as jnp
        import numpy as np
        NUM_EXPERTS = 4
        HIDDEN = 1024
        RANK = 8
        ALPHA = 8.0
        SCALE = ALPHA / RANK
        B, T, H = x.shape
        E = gate_w.shape[0]
        x_flat = x.reshape(-1, H)
        logits = x_flat @ gate_w.T + expert_bias
        top1 = jnp.argmax(logits, axis=-1)
        one_hot = jax.nn.one_hot(top1, E, dtype=x_flat.dtype)
        base_out = jnp.einsum('bth,oh->bto', x, W_up)
        z = jnp.einsum('nh,erh->ner', x_flat, lora_A)
        d = jnp.einsum('ner,ehr->neh', z, lora_B) * SCALE
        delta = jnp.einsum('neh,ne->nh', d, one_hot)
        return base_out + delta.reshape(B, T, H)
    x = x + _L0_xattn_ref(_layernorm(x, axis=-1), ctx_4096, L0_xattn_x1_scale, L0_xattn_x1_zp, L0_xattn_x2_scale, L0_xattn_x2_zp)
    x = x + _L0_ffn_ref(_layernorm(x, axis=-1), L0_ffn_W, L0_ffn_b, L0_ffn_A, L0_ffn_B, L0_ffn_router_W, L0_ffn_router_b)
    x = x + _L1_xattn_ref(_layernorm(x, axis=-1), ctx_4096, ctx_4096, mask_BxSxS2_ff0, L1_xattn_wq, L1_xattn_wk, L1_xattn_wv, L1_xattn_wo, 0)
    x = x + _L1_ffn_ref(_layernorm(x, axis=-1), L1_ffn_W_up, L1_ffn_gate_w, L1_ffn_expert_bias, L1_ffn_lora_A, L1_ffn_lora_B)
    return x

_drawn_inputs = setup_inputs


def setup_inputs(seed=0):
    import zlib

    import numpy as np

    out = dict(_drawn_inputs(seed))
    spreads = {'L1_ffn_expert_bias': (0.0, 2.0)}
    factors = {'L0_ffn_b': 24.141,
     'L0_ffn_A': 8.0,
     'L0_ffn_B': 8.0,
     'L0_ffn_router_W': 8.0,
     'L0_ffn_router_b': 8.0,
     'L1_xattn_wq': 8.0,
     'L1_xattn_wk': 8.0,
     'L1_xattn_wv': 3.705,
     'L1_xattn_wo': 3.743,
     'L1_ffn_gate_w': 8.0,
     'L1_ffn_lora_A': 8.0,
     'L1_ffn_lora_B': 8.0}
    for name, (base, spread) in spreads.items():
        noise = np.random.default_rng([zlib.crc32(name.encode()), seed]).standard_normal(out[name].shape)
        drawn = base * np.exp(spread * noise) if base else spread * noise
        out[name] = jnp.asarray(drawn.astype(out[name].dtype))
    for name, factor in factors.items():
        out[name] = (out[name] * factor).astype(out[name].dtype)
    return out
```

```python
from contextlib import ExitStack

import concourse.bass as bass
from concourse import mybir

F32 = mybir.dt.float32
F32R = mybir.dt.float32r
BF16 = mybir.dt.bfloat16
ALU = mybir.AluOpType
ACT = mybir.ActivationFunctionType
AX = mybir.AxisListType.X

MAGIC = 12582912.0
EPS = 1e-5
LOWEST = -3.4028234663852886e38
SP, PE, DV, AC, PO = "sync", "tensor", "vector", "scalar", "gpsimd"


class Queues:

    def __init__(self, nc, ctx):
        self.nc, self.ctx = nc, ctx
        self.q = {e: [] for e in (SP, PE, DV, AC, PO)}
        self.sems, self.count = {}, {}

    def op(self, eng, fn, w=(), s=None, inc=1):
        for name, value in w:
            self.q[eng].append((name, value, None))
        if s is None:
            self.q[eng].append((None, 0, fn))
            return None
        if s not in self.sems:
            self.sems[s] = self.ctx.enter_context(self.nc.semaphore(s))
            self.count[s] = 0
        self.count[s] += inc
        sem = self.sems[s]
        self.q[eng].append((None, 0, lambda e: fn(e).then_inc(sem, inc)))
        return (s, self.count[s])

    def dma(self, dst, src, w=(), s=None, eng=SP):
        return self.op(eng, lambda e: e.dma_start(dst, src), w, s, 16)

    def emit(self, eng, e):
        seen = {}
        for name, value, fn in self.q[eng]:
            if fn is not None:
                fn(e)
            elif seen.get(name, 0) < value:
                seen[name] = value
                e.wait_ge(self.sems[name], value)


def fl(ap):
    return ap.rearrange("p a b -> p (a b)")


def f32(ap):
    return ap.bitcast(F32)


def build(nc, A, out):
    with ExitStack() as ctx:
        build_in(nc, ctx, A, out)


def build_in(nc, ctx, A, out):
    Q = Queues(nc, ctx)
    op, dma = Q.op, Q.dma

    def alloc(stack, name, shape, dt=F32):
        return stack.enter_context(nc.sbuf_tensor(name, shape, dt))

    ps = ctx.enter_context(nc.psum_tensor("ps", [128, 8, 512], F32))
    k_d = nc.dram_tensor("k_scratch", [16, 128, 2, 1024], F32, kind="Internal").ap()
    v_d = nc.dram_tensor("v_scratch", [16, 128, 2, 1024], F32, kind="Internal").ap()
    h_d = nc.dram_tensor("h_scratch", [2, 128, 8, 2, 512], F32, kind="Internal").ap()
    x2_d = nc.dram_tensor("x2_scratch", [8, 128, 1024], F32, kind="Internal").ap()
    x3_d = nc.dram_tensor("x3_scratch", [8, 128, 1024], F32, kind="Internal").ap()

    def bank(b):
        return ps[:, b, :]

    def pair(b):
        return fl(ps[:, b:b + 2, :])

    def copy_hi(dst, src, w, s):
        return op(AC, lambda e: e.copy(dst, src), w, s)

    def sub_lo(eng, dst, src, hi, w, s):
        return op(eng, lambda e: e.tensor_tensor(dst, src, f32(hi), ALU.subtract), w, s)

    def tt(dst, a, b, o, w, s, eng=DV):
        return op(eng, lambda e: e.tensor_tensor(dst, a, b, o), w, s)

    def tsc(dst, a, s1, s2, o1, o2, w, s):
        if o2 is None:
            return op(DV, lambda e: e.tensor_scalar(dst, a, s1, None, o1), w, s)
        return op(DV, lambda e: e.tensor_scalar(dst, a, s1, s2, o1, o2), w, s)

    def stt(dst, a, sc, b, o1, o2, w, s):
        return op(DV, lambda e: e.scalar_tensor_tensor(out=dst, in0=a, scalar=sc, in1=b, op0=o1, op1=o2), w, s)

    def mm(dst, l, r, start, stop, w=(), s=None):
        return op(PE, lambda e: e.matmul(dst, l, r, start=start, stop=stop), w, s)

    def mm3(dst, lh, ll, rh, rl, start, stop, w=(), s=None):
        mm(dst, ll, rh, start, False, w)
        mm(dst, lh, rl, False, False)
        return mm(dst, lh, rh, False, stop, (), s)

    def transpose(dst, src, ident, w=(), s=None):
        return op(PE, lambda e: e.transpose(dst, src, ident), w, s)

    identf = alloc(ctx, "identf", [128, 128])
    sm = alloc(ctx, "sm", [128, 4, 20])
    scal = alloc(ctx, "scal", [128, 16])
    small = alloc(ctx, "small", [128, 64])
    t_id = dma(identf[:, :], A["identf"], (), "d_identf")

    ln_n = [0]

    def layernorm(x, dst, w, wdst, s):
        c = sm[:, ln_n[0] % 4, :]
        ln_n[0] += 1
        op(DV, lambda e: e.bn_stats(c[:, 0:6], x[:, 0:512]), w)
        t = op(DV, lambda e: e.bn_stats(c[:, 6:12], x[:, 512:1024]), (), "v_ln")
        t = op(DV, lambda e: e.bn_aggr(c[:, 12:14], c[:, 0:12]), [t], "v_ln")
        t = tsc(c[:, 14:15], c[:, 13:14], EPS, None, ALU.add, None, [t], "v_ln")
        t = op(AC, lambda e: e.activation(c[:, 15:16], c[:, 14:15], ACT.Sqrt), [t], "a_sqrt")
        t = op(DV, lambda e: e.reciprocal(c[:, 16:17], c[:, 15:16]), [t], "v_ln")
        t = tsc(c[:, 17:18], c[:, 16:17], c[:, 16:17], c[:, 14:15], ALU.mult, ALU.mult, [t], "v_ln")
        t = tsc(c[:, 18:19], c[:, 17:18], -0.5, 1.5, ALU.mult, ALU.add, [t], "v_ln")
        t = tsc(c[:, 19:20], c[:, 18:19], c[:, 16:17], None, ALU.mult, None, [t], "v_ln")
        return tsc(dst, x, c[:, 12:13], c[:, 19:20], ALU.subtract, ALU.mult, [t] + wdst, s)

    def rope(src, cos, sin, u, t, w, wu, s):
        tt(u, src, cos, ALU.mult, w + wu, None)
        tt(t[0:64], src[64:128], sin[64:128], ALU.mult, (), None)
        tok = tt(t[64:128], src[0:64], sin[0:64], ALU.mult, (), "v_rope")
        return tt(u, u, t, ALU.add, [tok], s), tok

    one = ExitStack()
    NC, NR = 9, 3
    ctxh = alloc(one, "ctxh", [128, NC, 1024], F32R)
    ctxl = alloc(one, "ctxl", [128, NC, 1024], F32R)
    raw = alloc(one, "raw", [128, NR, 1024])
    wh = alloc(one, "wh", [128, 2, 1024], F32R)
    wl = alloc(one, "wl", [128, 2, 1024], F32R)
    cosk = alloc(one, "cosk", [128, 1024])
    sink = alloc(one, "sink", [128, 1024])
    u_sb = alloc(one, "u_sb", [128, 2, 512])
    t_sb = alloc(one, "t_sb", [128, 512])
    khl = alloc(one, "khl", [128, 2, 2, 512], F32R)
    x_sb = alloc(one, "x_sb", [128, 8, 1024])
    ctab = alloc(one, "ctab", [128, 1024])
    tmp = alloc(one, "tmp", [128, 2, 1024])
    l0 = ExitStack()
    identb = alloc(l0, "identb", [128, 128], BF16)
    onesb = alloc(l0, "onesb", [128, 128], BF16)
    bq = alloc(l0, "bq", [128, 8, 1024], BF16)
    a1T = alloc(l0, "a1T", [128, 8, 512], BF16)
    a_sb = alloc(l0, "a_sb", [128, 2, 1024], BF16)

    free = {}

    def fr(key):
        return list(free.get(key, []))

    n_raw = [0]

    def load_split(src, hi, lo, w, eng=PO):
        r = n_raw[0] % NR
        n_raw[0] += 1
        d = dma(raw[:, r, :], src, fr(("raw", r)), f"d_raw{r}")
        h = copy_hi(hi, raw[:, r, :], [d] + w, "a_hi")
        l = sub_lo(eng, lo, raw[:, r, :], hi, [h] + w, "p_lo" if eng == PO else "v_lo")
        free[("raw", r)] = [l]
        return [h, l]

    tok_ctx = {}

    def load_ctx(b, k):
        i = b * 8 + k
        tok_ctx[i] = load_split(A["ctxT"][b, k], ctxh[:, i % NC, :], ctxl[:, i % NC, :],
                                fr(("c", i % NC)), DV if i % 2 else PO)

    units = [(b, g, kind) for b in range(2) for g in range(8) for kind in "kv"]
    tok_w = {}

    def load_w(n):
        if n >= len(units):
            return
        b, g, kind = units[n]
        tok_w[n] = load_split(A["wk" if kind == "k" else "wv"][g], wh[:, n % 2, :], wl[:, n % 2, :],
                              fr(("w", n % 2)))

    load_w(0)
    for k in range(8):
        load_ctx(0, k)
    t_cos = [dma(cosk[:, :], A["cosk"], (), "d_cosk"), dma(sink[:, :], A["sink"], (), "d_sink")]
    t_idb = [dma(identb[:, :], A["identb"], (), "d_identb"), dma(onesb[:, :], A["onesb"], (), "d_onesb")]
    t_sc = dma(scal[:, 0:4], A["scal"], (), "d_scal")
    t_x = {}
    for i in range(8):
        t_x[i] = [dma(x_sb[:, i, :], A["x"][i], (), f"d_x{i}")]

    tsc(scal[:, 6:7], scal[:, 1:2], -1.0, 128.0, ALU.mult, ALU.add, [t_sc], None)
    tsc(scal[:, 7:8], scal[:, 3:4], -1.0, 128.0, ALU.mult, ALU.add, (), None)
    op(DV, lambda e: e.reciprocal(scal[:, 4:5], scal[:, 0:1]))
    op(DV, lambda e: e.reciprocal(scal[:, 5:6], scal[:, 2:3]))
    t_s = tt(scal[:, 8:9], scal[:, 0:1], scal[:, 2:3], ALU.mult, (), "v_scal")
    t_s = tsc(scal[:, 9:10], scal[:, 6:7], scal[:, 7:8], 1024.0, ALU.mult, ALU.mult, [t_s], "v_scal")

    kv_n = [0]
    tok_kd, tok_vd = {}, {}
    late = []

    def kv_unit(n, half):
        b, g, kind = units[n]
        i = kv_n[0]
        kv_n[0] += 1
        bk = i % 4
        sl = n % 2
        for k in range(8):
            c = (b * 8 + k) % NC
            rh = ctxh[:, c, half * 512:half * 512 + 512]
            rl = ctxl[:, c, half * 512:half * 512 + 512]
            lh, ll = wh[:, sl, k * 128:k * 128 + 128], wl[:, sl, k * 128:k * 128 + 128]
            t = mm3(bank(bk), lh, ll, rh, rl, k == 0, k == 7,
                    tok_w[n] + tok_ctx[b * 8 + k] + (fr(("b", bk)) if k == 0 else []),
                    "t_kv" if k == 7 or (n % 16 == 15 and half == 1) else None)
            if n % 16 == 15 and half == 1:
                free[("c", c)] = [t]
        free[("w", sl)] = [t]
        o = i % 2
        u = u_sb[:, o, :]
        if kind == "k":
            tu, tt_ = rope(bank(bk), cosk[:, half * 512:half * 512 + 512], sink[:, half * 512:half * 512 + 512],
                           u, t_sb[:, :], [t] + t_cos, fr(("u", o)), "v_kr")
            free[("b", bk)] = [tt_]
            th = copy_hi(khl[:, o, 0, :], u, [tu] + fr(("khl", o)), "a_khi")
            tl = sub_lo(DV, khl[:, o, 1, :], u, khl[:, o, 0, :], [th] + fr(("khl", o)), "v_klo")
            free[("u", o)] = [tl]
            td = dma(k_d[b * 8 + g, :, :, half * 512:half * 512 + 512], f32(khl[:, o, :, :]), [tl], f"d_khl{o}")
            free[("khl", o)] = [td]
            tok_kd.setdefault(b * 8 + g, []).append(td)
        else:
            tu = op(AC, lambda e: e.copy(u, bank(bk)), [t] + fr(("u", o)), "a_vt")
            free[("b", bk)] = [tu]

            def finish():
                for j in range(4):
                    t2 = transpose(ps[:, 6, j * 128:j * 128 + 128], u[:, j * 128:j * 128 + 128], identf[:, :],
                                   [tu, t_id] + fr(("b", 6)), "t_vtr" if j == 3 else None)
                free[("u", o)] = [t2]
                th = copy_hi(khl[:, o, 0, :], bank(6), [t2] + fr(("khl", o)), "a_khi")
                tl = sub_lo(DV, khl[:, o, 1, :], bank(6), khl[:, o, 0, :], [th] + fr(("khl", o)), "v_klo")
                free[("b", 6)] = [tl]
                td = dma(v_d[b * 8 + g, :, :, half * 512:half * 512 + 512], f32(khl[:, o, :, :]), [tl], f"d_khl{o}")
                free[("khl", o)] = [td]
                tok_vd.setdefault(b * 8 + g, []).append(td)

            late.append(finish)

    n_tmp, n_a = [0], [0]
    R = small[:, 0:8]

    def quantise(src, rs, z, dst, w, wd, s):
        k = n_tmp[0] % 2
        n_tmp[0] += 1
        q = tmp[:, k, :]
        t = tsc(q, src, scal[:, rs:rs + 1], scal[:, z:z + 1], ALU.mult, ALU.add, w + fr(("tmp", k)), "v_q")
        t2 = tsc(q, q, MAGIC, MAGIC, ALU.add, ALU.max, [t], "v_q")
        t3 = tsc(dst, q, MAGIC + 255.0, -(MAGIC + 128.0), ALU.min, ALU.add, [t2] + wd, s)
        free[("tmp", k)] = [t3]
        return t, t3

    def background_l0(b):
        pend = []

        def flush():
            while pend:
                pend.pop(0)()

        for i in range(4):
            tile = b * 4 + i
            k = n_tmp[0] % 2
            n_tmp[0] += 1
            th = layernorm(x_sb[:, tile, :], tmp[:, k, :], t_x[tile], fr(("tmp", k)), "v_h")
            a = n_a[0] % 2
            n_a[0] += 1
            tq, ta = quantise(tmp[:, k, :], 4, 1, a_sb[:, a, :], [th, t_s], fr(("a", a)), "v_a")
            free[("tmp", k)] = [tq]
            t = op(DV, lambda e, a=a, tile=tile: e.reduce_sum(R[:, tile:tile + 1], a_sb[:, a, :], AX), [ta], "v_rs")
            tsc(R[:, tile:tile + 1], R[:, tile:tile + 1], scal[:, 7:8], None, ALU.mult, None, [t], "v_rs")

            def tr(i=i, a=a, ta=ta):
                pb = bank(7).bitcast(BF16)
                for k8 in range(8):
                    t = transpose(pb[:, k8 * 128:k8 * 128 + 128], a_sb[:, a, k8 * 128:k8 * 128 + 128], identb[:, :],
                                  [ta] + t_idb + fr(("b", 7)), "t_atr" if k8 == 7 else None)
                free[("a", a)] = [t]
                t = op(AC, lambda e: e.copy(a1T[:, :, i * 128:i * 128 + 128],
                                            pb.rearrange("p (k t) -> p k t", k=8)),
                       [t] + fr("a1T"), "a_a1T")
                free[("b", 7)] = [t]
                tok_a1T.append(t)

            yield
            flush()
            pend.append(tr)
        for k in range(8):
            r = n_raw[0] % NR
            n_raw[0] += 1
            d = dma(raw[:, r, :], A["ctx"][b, k], fr(("raw", r)), f"d_raw{r}")
            t1, tq = quantise(raw[:, r, :], 5, 3, bq[:, k, :], [d, t_s], fr("bq"), "v_bq")
            free[("raw", r)] = [t1]
            tok_bq[k] = tq
            yield
            flush()

    tok_a1T, tok_bq = [], {}

    def l0_product(b):
        w = list(tok_a1T) + list(tok_bq.values()) + t_idb
        for nh in range(2):
            for k in range(8):
                t = mm(bank(4 + nh), onesb[:, :], bq[:, k, nh * 512:nh * 512 + 512], k == 0, k == 7,
                       w + fr(("b", 4 + nh)), "t_l0" if k == 7 else None)
            t = tsc(ctab[:, nh * 512:nh * 512 + 512], bank(4 + nh), scal[:, 6:7], scal[:, 9:10], ALU.mult, ALU.add,
                    [t], "v_ctab")
            free[("b", 4 + nh)] = [t]
            t_c = t
        n = 0
        for i in range(4):
            tile = b * 4 + i
            for nh in range(2):
                bk = 4 + n % 2
                n += 1
                for k in range(8):
                    t = mm(bank(bk), a1T[:, k, i * 128:i * 128 + 128], bq[:, k, nh * 512:nh * 512 + 512],
                           k == 0, k == 7, fr(("b", bk)), "t_l0" if k == 7 else None)
                kk = n_tmp[0] % 2
                n_tmp[0] += 1
                q = tmp[:, kk, 0:512]
                xs = x_sb[:, tile, nh * 512:nh * 512 + 512]
                t2 = stt(q, bank(bk), R[:, tile:tile + 1], ctab[:, nh * 512:nh * 512 + 512], ALU.add, ALU.add,
                         [t, t_c] + fr(("tmp", kk)), "v_l0")
                free[("b", bk)] = [t2]
                t3 = stt(xs, q, scal[:, 8:9], xs, ALU.mult, ALU.add, [t2], "v_l0")
                free[("tmp", kk)] = [t3]
            t_x[tile] = [t3]
        free["bq"] = free["a1T"] = [t]
        tok_a1T.clear()
        free["ctab"] = [t2]
        return t

    def run_kv(ns, bg, per=1):
        for n in ns:
            load_w(n + 1)
            for half in range(2):
                kv_unit(n, half)
                if len(late) > 1 or (late and units[n][2] == "k"):
                    late.pop(0)()
                for _ in range(per):
                    if bg is not None:
                        next(bg, None)

    run_kv(range(0, 16), background_l0(0))
    while late:
        late.pop(0)()
    for k in range(8):
        load_ctx(1, k)
    l0_product(0)
    run_kv(range(16, 24), background_l0(1))
    t_l0 = l0_product(1)
    l0.close()
    h2h = alloc(one, "h2h", [128, 8, 512], F32R)
    h2l = alloc(one, "h2l", [128, 8, 512], F32R)
    w_h2 = [t_l0]
    t_bias = dma(ctab[:, :], A["bias"], fr("ctab"), "d_bias")
    tok_h2 = {}

    def ffn_norm(tile):
        k = n_tmp[0] % 2
        n_tmp[0] += 1
        t = layernorm(x_sb[:, tile, :], tmp[:, k, :], t_x[tile], fr(("tmp", k)), "v_h")
        t_x[tile] = [tt(x_sb[:, tile, :], x_sb[:, tile, :], ctab[:, :], ALU.add, [t, t_bias], "p_xb", eng=PO)]
        return k, t

    def tile_transposes(k, t, w=()):
        for j in range(8):
            t2 = transpose(ps[:, 4 + j // 4, (j % 4) * 128:(j % 4) * 128 + 128], tmp[:, k, j * 128:j * 128 + 128],
                           identf[:, :], [t, t_id] + (fr(("b", 4)) + fr(("b", 5)) if j == 0 else []),
                           "t_htr" if j == 7 else None)
        free[("tmp", k)] = [t2]
        return t2

    def ffn_transposes(tile, k, t):
        i = tile % 4
        t2 = tile_transposes(k, t)
        dst = h2h[:, :, i * 128:i * 128 + 128]
        src = pair(4).rearrange("p (k t) -> p k t", k=8)
        w = w_h2 + fr(("h2", i))
        th = copy_hi(dst, src, [t2] + w, "a_h2")
        tl = sub_lo(DV, h2l[:, :, i * 128:i * 128 + 128], src, dst, [th] + w, "v_h2")
        free[("b", 4)] = free[("b", 5)] = [tl]
        tok_h2[i] = [th, tl]

    def background_ffn():
        for i in range(4):
            k, t = ffn_norm(i)
            yield
            ffn_transposes(i, k, t)
            yield

    run_kv(range(24, 32), background_ffn())
    while late:
        late.pop(0)()

    tok_A = load_split(A["loraA"], wh[:, 0, :], wl[:, 0, :], fr(("w", 0)))
    tok_W = {}
    for k in range(8):
        i = 16 + k
        tok_W[k] = load_split(A["W"][k], ctxh[:, i % NC, :], ctxl[:, i % NC, :], fr(("c", i % NC)),
                              DV if i % 2 else PO)
        if k == 1:
            tok_B = load_split(A["loraB"], wh[:, 1, :], wl[:, 1, :], fr(("w", 1)))
    rw = cosk[:, 0:64]
    w_cos = [t for t in free[("b", 0)] + free[("b", 1)] + free[("b", 2)] + free[("b", 3)]]
    t_rt = [dma(rw, A["rw"], w_cos, "d_rw"), dma(small[:, 40:56], A["rb"], (), "d_rb")]
    qbc = sink[:, :]
    tok_ts = {}

    def lora_t(b):
        for k in range(8):
            t = mm3(bank(6), wh[:, 0, k * 128:k * 128 + 128], wl[:, 0, k * 128:k * 128 + 128], h2h[:, k, :],
                    h2l[:, k, :], k == 0, k == 7,
                    tok_A + [x for v in tok_h2.values() for x in v] + (fr(("b", 6)) if k == 0 else []),
                    "t_lt" if k == 7 else None)
        return t

    def router(b):
        w = [x for v in tok_h2.values() for x in v]
        op(DV, lambda e: e.tensor_reduce(small[:, 8:16], f32(h2h[:, :, 179:511]), AX, ALU.add), w)
        t = op(DV, lambda e: e.tensor_reduce(small[:, 16:24], f32(h2l[:, :, 179:511]), AX, ALU.add), (), "v_rt")
        t = tt(small[:, 8:16], small[:, 8:16], small[:, 16:24], ALU.add, [t], "v_rt")
        t = op(DV, lambda e: e.tensor_copy(qbc.rearrange("p (k m) -> p k m", k=8),
                                           small[:, 8:16].unsqueeze(2).broadcast_to([128, 8, 128])),
               [t] + w_cos + fr("qbc"), "v_rt")
        for k in range(8):
            t2 = mm(ps[:, 7, 0:8], qbc[:, k * 128:k * 128 + 128], rw[:, k * 8:k * 8 + 8], k == 0, k == 7,
                    [t] + t_rt + fr(("b", 7)), "t_rt" if k == 7 else None)
        free["qbc"] = [t2]
        t = stt(small[:, 16:24], ps[:, 7, 0:8], 1.0 / 332.0, small[:, 40:48], ALU.mult, ALU.add, [t2], "v_rt")
        free[("b", 7)] = [t]
        t = op(DV, lambda e: e.reduce_max(small[:, 32:33], small[:, 16:24], AX), [t], "v_rt")
        t = tsc(small[:, 33:34], small[:, 32:33], -1.0, None, ALU.mult, None, [t], "v_rt")
        t = op(AC, lambda e: e.activation(small[:, 24:32], small[:, 16:24], ACT.Exp, bias=small[:, 33:34],
                                          accum_out=small[:, 34:35]), [t], "a_rt")
        t = op(DV, lambda e: e.reciprocal(small[:, 35:36], small[:, 34:35]), [t], "v_rt")
        t = op(DV, lambda e: e.tensor_tensor_reduce(out=small[:, 56:64], in0=small[:, 24:32], in1=small[:, 48:56],
                                                    scale=2.0, scalar=0.0, op0=ALU.mult, op1=ALU.add,
                                                    accum_out=small[:, 36:37]), [t], "v_rt")
        return tsc(small[:, 37 + b:38 + b], small[:, 36:37], small[:, 35:36], None, ALU.mult, None, [t], "v_rt")

    def lora_scale(b, t, tr):
        u = u_sb[:, 0, :]
        t2 = tsc(u, bank(6), small[:, 37 + b:38 + b], None, ALU.mult, None, [t, tr] + fr(("u", 0)), "v_ts")
        free[("b", 6)] = [t2]
        ts = ts_sb[b]
        th = copy_hi(ts[:, 0, :], u, [t2] + w_ts, "a_ts")
        tl = sub_lo(DV, ts[:, 1, :], u, ts[:, 0, :], [th] + w_ts, "v_tl")
        free[("u", 0)] = [tl]
        tok_ts[b] = [th, tl]

    ts0 = alloc(one, "ts0", [128, 2, 512], F32R)
    ts_sb = [ts0, ts0]
    w_ts = []
    tok_x2, tok_hd = {}, {}

    def ffn_main(i, k, nh, bk, w=()):
        c = (16 + k) % NC
        return mm3(bank(bk), h2h[:, k, i * 128:i * 128 + 128], h2l[:, k, i * 128:i * 128 + 128],
                   ctxh[:, c, nh * 512:nh * 512 + 512], ctxl[:, c, nh * 512:nh * 512 + 512], k == 0, False,
                   tok_W[k] + tok_h2[i] + list(w), "t_fm" if k == 7 else None)

    def ffn_lora(b, i, nh, bk):
        ts = ts_sb[b]
        return mm3(bank(bk), ts[:, 0, i * 128:i * 128 + 128], ts[:, 1, i * 128:i * 128 + 128],
                   wh[:, 1, nh * 512:nh * 512 + 512], wl[:, 1, nh * 512:nh * 512 + 512], False, True,
                   tok_B + tok_ts[b], "t_fl")

    n_khl = [0]

    def ffn_end(b, i, bks, ts):
        tile = b * 4 + i
        for nh in range(2):
            xs = x_sb[:, tile, nh * 512:nh * 512 + 512]
            t = tt(xs, bank(bks[nh]), xs, ALU.add, [ts[nh]] + t_x[tile], "v_x2")
            free[("b", bks[nh])] = [t]
        tok_x2[tile] = dma(x2_d[tile], x_sb[:, tile, :], [t], f"d_x{tile}")
        k = n_tmp[0] % 2
        n_tmp[0] += 1
        t = layernorm(x_sb[:, tile, :], tmp[:, k, :], [t], fr(("tmp", k)), "v_h")

        def finish():
            t2 = tile_transposes(k, t)
            for j in range(2):
                th = copy_hi(khl[:, j, 0, :], bank(4 + j), [t2] + fr(("khl", j)), "a_khi")
                tl = sub_lo(DV, khl[:, j, 1, :], bank(4 + j), khl[:, j, 0, :], [th], "v_klo")
                free[("b", 4 + j)] = [tl]
                for hl in range(2):
                    td = dma(h_d[b, :, 4 * j:4 * j + 4, hl, i * 128:i * 128 + 128],
                             f32(khl[:, j, hl, :]).rearrange("p (k t) -> p k t", k=4), [tl], f"d_khl{j}")
                free[("khl", j)] = [td]
                tok_hd.setdefault(b, []).append(td)

        return finish

    t_lt = lora_t(0)
    t_r = router(0)
    lora_scale(0, t_lt, t_r)
    for k in range(8):
        for i in range(2):
            for nh in range(2):
                ffn_main(i, k, nh, 2 * i + nh, fr(("b", 2 * i + nh)) if k == 0 else ())
    fin = None
    for i in range(2):
        tl = [ffn_lora(0, i, nh, 2 * i + nh) for nh in range(2)]
        free[("h2", i)] = [tl[1]]
        f = ffn_end(0, i, [2 * i, 2 * i + 1], tl)
        if fin:
            fin()
        fin = f

    def ffn_tile(b, i, bks, between=()):
        nonlocal fin
        for nh in range(2):
            for k in range(8):
                t = ffn_main(i, k, nh, bks[nh], fr(("b", bks[nh])) if k == 0 else ())
            if nh == 0:
                if fin:
                    fin()
                    fin = None
                for f in between:
                    f()
        free[("h2", i)] = [t]
        tl = [ffn_lora(b, i, nh, bks[nh]) for nh in range(2)]
        if i == 3 and b == 0:
            w_ts.append(tl[1])
        fin = ffn_end(b, i, bks, tl)

    held = {}

    def norm_next(i):
        def f():
            held[i] = ffn_norm(4 + i)
        return f

    def trans_next(i):
        def f():
            ffn_transposes(4 + i, *held[i])
        return f

    ffn_tile(0, 2, [0, 1], [norm_next(0)])
    trans_next(0)()
    norm_next(1)()
    trans_next(1)()
    ffn_tile(0, 3, [2, 3], [norm_next(2)])
    trans_next(2)()
    norm_next(3)()
    trans_next(3)()
    t_lt = lora_t(1)
    t_r = router(1)
    lora_scale(1, t_lt, t_r)
    for i in range(4):
        ffn_tile(1, i, [2 * (i % 2), 2 * (i % 2) + 1])
    fin()

    edge = [("t_htr", Q.count["t_htr"]), ("t_fl", Q.count["t_fl"]), ("v_klo", Q.count["v_klo"]),
            ("a_khi", Q.count["a_khi"]), ("p_lo", Q.count["p_lo"]), ("p_xb", Q.count["p_xb"]),
            ("d_khl0", Q.count["d_khl0"]), ("d_khl1", Q.count["d_khl1"])]
    edge += [tok_x2[i] for i in range(8)]
    one.close()
    free.clear()

    two = ExitStack()
    hT = alloc(two, "hT", [128, 8, 2, 512], F32R)
    xa = alloc(two, "xa", [128, 4, 1024])
    mask = alloc(two, "mask", [128, 4, 1024])
    cosq = alloc(two, "cosq", [128, 512])
    sinq = alloc(two, "sinq", [128, 512])
    ksb = alloc(two, "ksb", [128, 2, 2, 1024], F32R)
    vsb = alloc(two, "vsb", [128, 2, 1024], F32R)
    qsb = alloc(two, "qsb", [128, 2, 2, 512], F32R)
    psb = alloc(two, "psb", [128, 3, 1024])
    pth = alloc(two, "pth", [128, 8, 512], F32R)
    ptl = alloc(two, "ptl", [128, 8, 512], F32R)
    osb = alloc(two, "osb", [128, 2, 2, 2, 512], F32R)
    araw = alloc(two, "araw", [128, 4, 512])
    wqh = alloc(two, "wqh", [128, 3, 512], F32R)
    wql = alloc(two, "wql", [128, 3, 512], F32R)
    woh = alloc(two, "woh", [128, 2, 2, 512], F32R)
    wol = alloc(two, "wol", [128, 2, 2, 512], F32R)
    ua = alloc(two, "ua", [128, 512])
    ta = alloc(two, "ta", [128, 512])
    rb = alloc(two, "rb", [128, 512])
    st = alloc(two, "st", [128, 4, 16])

    n_ar = [0]

    def load_split2(src, hi, lo, w):
        r = n_ar[0] % 4
        n_ar[0] += 1
        d = dma(araw[:, r, :], src, fr(("ar", r)) + edge, f"d_ar{r}")
        h = copy_hi(hi, araw[:, r, :], [d] + w, "a_whi")
        l = sub_lo(PO, lo, araw[:, r, :], hi, [h] + w, "p_wlo")
        free[("ar", r)] = [l]
        return [h, l]

    tok_wq, tok_wo, tok_q, tok_h3 = {}, {}, {}, {}

    def load_wq(n):
        if n >= 128:
            return
        head, half = (n // 2) % 32, n % 2
        sl = n % 3
        tok_wq[n] = load_split2(A["wq"][head, :, half * 512:half * 512 + 512], wqh[:, sl, :], wql[:, sl, :],
                                fr(("wq", sl)))

    def load_wo(q):
        j, nh = (q - 2) // 2, q % 2
        if q < 2 or j >= 32:
            return
        tok_wo[q] = []
        for i in range(2):
            head = (2 * j + i) % 32
            tok_wo[q] += load_split2(A["wo"][head, :, nh * 512:nh * 512 + 512], woh[:, nh, i, :], wol[:, nh, i, :],
                                     fr(("wo", nh)))

    def load_h(b, w, wt):
        tok_h3[(b, w)] = dma(f32(hT[:, 2 * w:2 * w + 2, :, :]), h_d[b, :, 2 * w:2 * w + 2, :, :], tok_hd[b] + wt, f"d_h{w}")

    tok_k, tok_v, tok_m, tok_xa = {}, {}, {}, {}

    def load_k(G):
        if G < 16:
            tok_k[G] = dma(f32(ksb[:, G % 2, :, :]), k_d[G], tok_kd[G] + fr(("k", G % 2)) + edge, f"d_k{G % 2}")

    def load_v(G):
        if G < 16:
            tok_v[G] = dma(f32(vsb[:, :, :]), v_d[G], tok_vd[G] + fr("v") + edge, "d_v")

    def load_mask(b, i, w):
        tok_m[(b, i)] = dma(mask[:, i, :], A["mask"][b * 4 + i], w, f"d_m{i}")

    load_wq(0)
    for w in range(4):
        load_h(0, w, edge)
        if w == 0:
            load_wq(1)
            t_cq = [dma(cosq[:, :], A["cosq"], edge, "d_cosq"), dma(sinq[:, :], A["sinq"], edge, "d_sinq")]
    load_wq(2)
    load_k(0)
    load_mask(0, 0, edge)
    load_v(0)
    for i in range(1, 4):
        load_mask(0, i, edge)
    for i in range(4):
        tok_xa[(0, i)] = dma(xa[:, i, :], x2_d[i], [tok_x2[i]] + edge, f"d_xa{i}")

    def q_part(H, w):
        b = H // 32
        for k in (2 * w, 2 * w + 1):
            n = 2 * H + k // 4
            sl = n % 3
            c = (k % 4) * 128
            t = mm3(bank(5), wqh[:, sl, c:c + 128], wql[:, sl, c:c + 128], hT[:, k, 0, :], hT[:, k, 1, :],
                    k == 0, k == 7, tok_wq[n] + [tok_h3[(b, w)]] + (fr("q_bank") if k == 0 else []),
                    "t_q" if k % 2 else None)
        if w % 2:
            free[("wq", (2 * H + w // 2) % 3)] = [t]
        if H == 31:
            load_h(1, w, [t])
        return t

    def q_end(H, t):
        o = H % 2
        tu, tr = rope(bank(5), cosq[:, :], sinq[:, :], ua[:, :], ta[:, :], [t] + t_cq, fr("ua"), "v_qr")
        free["q_bank"] = [tr]
        w = fr(("q", o))
        th = copy_hi(qsb[:, o, 0, :], ua[:, :], [tu] + w, "a_qhi")
        tl = sub_lo(DV, qsb[:, o, 1, :], ua[:, :], qsb[:, o, 0, :], [th] + w, "v_qlo")
        free["ua"] = [tl]
        tok_q[H] = [th, tl]

    n_p = [0]
    tok_p, tok_pt, tok_sum = {}, {}, {}

    def scores(H, i):
        b, G, o = H // 32, H // 4, H % 2
        for nh in range(2):
            t = mm3(bank(nh), qsb[:, o, 0, i * 128:i * 128 + 128], qsb[:, o, 1, i * 128:i * 128 + 128],
                    ksb[:, G % 2, 0, nh * 512:nh * 512 + 512], ksb[:, G % 2, 1, nh * 512:nh * 512 + 512], True, True,
                    tok_q[H] + [tok_k[G]] + fr("s_bank"), "t_s" if nh else None)
        if i == 3:
            free[("q", o)] = [t]
            if H % 4 == 3:
                free[("k", G % 2)] = [t]
        r = n_p[0] % 3
        n_p[0] += 1
        P = psb[:, r, :]
        c = st[:, H % 4, :]
        tm = op(DV, lambda e: e.tensor_tensor_reduce(out=P, in0=pair(0), in1=mask[:, i, :], scale=1.0,
                                                     scalar=LOWEST, op0=ALU.add, op1=ALU.max,
                                                     accum_out=c[:, i:i + 1]),
                [t, tok_m[(b, i)]] + fr(("p", r)), "v_max")
        free["s_bank"] = [tm]
        if H == 31:
            load_mask(1, i, [tm])
        tn = tsc(c[:, 4 + i:5 + i], c[:, i:i + 1], -1.0, None, ALU.mult, None, [tm], "v_nmax")
        te = op(AC, lambda e: e.activation(P, P, ACT.Exp, bias=c[:, 4 + i:5 + i], accum_out=c[:, 8 + i:9 + i]),
                [tn, tm], "a_exp")
        tok_p[(H, i)] = (r, te)

    def p_transposes(H, i):
        r, te = tok_p[(H, i)]
        for k in range(8):
            t = transpose(ps[:, 2 + k // 4, (k % 4) * 128:(k % 4) * 128 + 128], psb[:, r, k * 128:k * 128 + 128],
                          identf[:, :], [te] + fr("t_bank"), "t_p" if k == 7 else None)
        free[("p", r)] = [t]
        src = pair(2).rearrange("p (k t) -> p k t", k=8)
        w = fr("pt")
        th = copy_hi(pth[:, :, i * 128:i * 128 + 128], src, [t] + w, "a_pt")
        tl = sub_lo(DV, ptl[:, :, i * 128:i * 128 + 128], src, pth[:, :, i * 128:i * 128 + 128], [th] + w, "v_pt")
        free["t_bank"] = [tl]
        tok_pt[(H, i)] = [th, tl]

    tok_rb = {}

    def inverse_rows(H):
        c = st[:, H % 4, :]
        t = op(DV, lambda e: e.reciprocal(c[:, 12:16], c[:, 8:12]), [tok_p[(H, 3)][1]], "v_rinv")
        for i in range(4):
            t2 = transpose(ps[:, 7, i * 128:i * 128 + 128], c[:, 12 + i:13 + i].broadcast_to([128, 128]),
                           identf[:, :], [t] + fr("rb_bank"), "t_rb" if i == 3 else None)
        t3 = op(AC, lambda e: e.copy(rb[:, :], bank(7)), [t2] + fr("rb"), "a_rb")
        free["rb_bank"] = [t3]
        tok_rb[H] = t3

    def values(H):
        w = [x for i in range(4) for x in tok_pt[(H, i)]] + [tok_v[H // 4]] + fr("o_bank")
        for k in range(8):
            t = mm3(bank(4), vsb[:, 0, k * 128:k * 128 + 128], vsb[:, 1, k * 128:k * 128 + 128],
                    pth[:, k, :], ptl[:, k, :], k == 0, k == 7, w, "t_av" if k == 7 else None)
        free["pt"] = [t]
        if H % 4 == 3:
            free["v"] = [t]
        return t

    tok_o = {}

    def o_scale(H, t):
        t2 = tt(ta[:, :], bank(4), rb[:, :], ALU.mult, [t, tok_rb[H]] + fr("ta"), "v_o")
        free["o_bank"] = free["rb"] = [t2]
        return t2

    def o_split(H, t2):
        j, i = (H // 2) % 2, H % 2
        w = fr(("o", j))
        th = copy_hi(osb[:, j, i, 0, :], ta[:, :], [t2] + w, "a_o")
        tl = sub_lo(DV, osb[:, j, i, 1, :], ta[:, :], osb[:, j, i, 0, :], [th] + w, "v_olo")
        free["ta"] = [tl]
        tok_o[H] = [th, tl]

    tok_x3 = {}

    def wo_part(q, i):
        j, nh = (q - 2) // 2, q % 2
        if q < 2 or j >= 32:
            return
        b = j // 16
        for hd in range(2):
            t = mm3(bank(6), osb[:, j % 2, hd, 0, i * 128:i * 128 + 128], osb[:, j % 2, hd, 1, i * 128:i * 128 + 128],
                    woh[:, nh, hd, :], wol[:, nh, hd, :], hd == 0, hd == 1,
                    tok_wo[q] + tok_o[2 * j] + tok_o[2 * j + 1] + (fr("wo_bank") if hd == 0 else []),
                    "t_wo" if hd else None)
        if i == 3:
            free[("wo", nh)] = [t]
            if nh:
                free[("o", j % 2)] = [t]
        xs = xa[:, i, nh * 512:nh * 512 + 512]
        t = tt(xs, bank(6), xs, ALU.add, [t, tok_xa[(b, i)]], "v_xa")
        free["wo_bank"] = [t]
        if j % 16 == 15 and nh:
            tok_x3[b * 4 + i] = dma(x3_d[b * 4 + i], xa[:, i, :], [t], f"d_xs{i}")
            if b == 0:
                tok_xa[(1, i)] = dma(xa[:, i, :], x2_d[4 + i], [tok_x3[i], tok_x2[4 + i]], f"d_xa{i}")

    for p in range(-2, 66):
        has = 0 <= p < 64
        if has and p % 4 == 0:
            load_k(p // 4 + 1)
        if p + 2 >= 1:
            load_wq(2 * (p + 2) + 2) if p > -2 else None
        load_wo(p + 1)
        if has:
            scores(p, 0)
        if 1 <= p <= 64:
            t = values(p - 1)
            t2 = o_scale(p - 1, t)
            if (p - 1) % 4 == 3:
                load_v((p - 1) // 4 + 1)
        if has:
            scores(p, 1)
        if 1 <= p <= 64:
            o_split(p - 1, t2)
        for w in range(4):
            if has:
                p_transposes(p, w)
            if w == 3 and has:
                inverse_rows(p)
            if p + 2 < 64:
                tq = q_part(p + 2, w)
                if w == 1:
                    load_wq(2 * (p + 2) + 3)
            wo_part(p, w)
            if has and w < 2:
                scores(p, w + 2)
        if p + 2 < 64:
            q_end(p + 2, tq)

    edge2 = [("t_wo", Q.count["t_wo"]), ("v_xa", Q.count["v_xa"]), ("a_o", Q.count["a_o"]),
             ("p_wlo", Q.count["p_wlo"]), ("v_olo", Q.count["v_olo"])] + [tok_x3[i] for i in range(8)]
    two.close()
    free.clear()

    three = ExitStack()
    uph = alloc(three, "uph", [128, 8, 1024], F32R)
    upl = alloc(three, "upl", [128, 8, 1024], F32R)
    raw3 = alloc(three, "raw3", [128, 4, 1024])
    x3 = alloc(three, "x3", [128, 3, 1024])
    ag_raw = alloc(three, "ag_raw", [128, 288])
    agh = alloc(three, "agh", [128, 8, 36], F32R)
    agl = alloc(three, "agl", [128, 8, 36], F32R)
    lbr = alloc(three, "lbr", [128, 1024])
    lbh = alloc(three, "lbh", [128, 1024], F32R)
    lbl = alloc(three, "lbl", [128, 1024], F32R)
    h4 = alloc(three, "h4", [128, 2, 1024])
    h4h = alloc(three, "h4h", [128, 2, 8, 128], F32R)
    h4l = alloc(three, "h4l", [128, 2, 8, 128], F32R)
    zs = alloc(three, "zs", [128, 2, 128])
    zth = alloc(three, "zth", [128, 2, 128], F32R)
    ztl = alloc(three, "ztl", [128, 2, 128], F32R)
    g_sb = alloc(three, "g_sb", [128, 2, 32])
    eb = alloc(three, "eb", [128, 8])
    y = alloc(three, "y", [128, 2, 1024])

    t_ag = dma(ag_raw[:, :], A["ag"], edge2, "d_ag")
    t_eb = dma(eb[:, :], A["eb"], edge2, "d_eb")
    t_lbz = op(DV, lambda e: e.memset(lbr[:, :], 0.0), edge2, "v_lbz")
    t_zz = op(DV, lambda e: e.memset(zs[:, :, :], 0.0), edge2, "v_zz")
    t_lb = dma(lbr[0:32, :], A["lb"], [t_lbz], "d_lb")
    agf = agh[:, :, :].rearrange("p a b -> p (a b)")
    agf2 = agl[:, :, :].rearrange("p a b -> p (a b)")
    th = copy_hi(agf, ag_raw[:, :], [t_ag], "a_ag")
    tok_ag = [th, sub_lo(DV, agf2, ag_raw[:, :], agf, [th], "v_ag")]
    tok_up = {}

    def load_x3(i):
        sl = i % 3
        t_x3[i] = dma(x3[:, sl, :], x3_d[i], [tok_x3[i]] + edge2 + fr(("x3", sl)), f"d_x3{sl}")

    t_x3 = {}
    load_x3(0)
    load_x3(1)
    n3 = [0]

    def load_up(k):
        r = n3[0] % 4
        n3[0] += 1
        d = dma(raw3[:, r, :], A["up"][k], fr(("r3", r)) + edge2, f"d_r3{r}")
        h = copy_hi(uph[:, k, :], raw3[:, r, :], [d], "a_up")
        eng = DV if k % 2 else PO
        l = sub_lo(eng, upl[:, k, :], raw3[:, r, :], uph[:, k, :], [h], "v_up" if k % 2 else "p_up")
        free[("r3", r)] = [l]
        tok_up[k] = [h, l]

    tok_h4, tok_z, tok_zt = {}, {}, {}

    def norm3(i):
        sl = i % 2
        if i + 2 < 8 and i > 0:
            pass
        return layernorm(x3[:, i % 3, :], h4[:, sl, :], [t_x3[i]] + edge2, fr(("h4", sl)), "v_h4")

    def trans3(i, t):
        sl = i % 2
        for j in range(8):
            t2 = transpose(ps[:, 4 + j // 4, (j % 4) * 128:(j % 4) * 128 + 128], h4[:, sl, j * 128:j * 128 + 128],
                           identf[:, :], [t] + fr("b45"), "t_h4" if j == 7 else None)
        free[("h4", sl)] = [t2]
        src = pair(4).rearrange("p (k t) -> p k t", k=8)
        w = fr(("h4t", sl))
        th = copy_hi(h4h[:, sl, :, :], src, [t2] + w, "a_h4")
        tl = sub_lo(DV, h4l[:, sl, :, :], src, h4h[:, sl, :, :], [th] + w, "v_h4l")
        free["b45"] = [tl]
        tok_h4[i] = [th, tl]

    def gate(i):
        sl = i % 2
        for k in range(8):
            t = mm3(ps[:, 6, 0:36], h4h[:, sl, k, :], h4l[:, sl, k, :], agh[:, k, :], agl[:, k, :], k == 0, k == 7,
                    tok_h4[i] + tok_ag + fr("b6"), "t_g" if k == 7 else None)
        g = g_sb[:, sl, :]
        t = tt(g[:, 0:4], ps[:, 6, 32:36], eb[:, 0:4], ALU.add, [t, t_eb] + fr(("g", sl)), "v_g")
        t = op(DV, lambda e: e.reduce_max(g[:, 4:5], g[:, 0:4], AX), [t], "v_g")
        t = tsc(g[:, 8:12], g[:, 0:4], g[:, 4:5], None, ALU.is_equal, None, [t], "v_g")
        t = op(DV, lambda e: e.tensor_tensor_scan(g[:, 12:16], eb[:, 4:8], g[:, 8:12], 0.0, ALU.mult, ALU.add),
               [t], "v_g")
        t = stt(g[:, 16:20], g[:, 12:16], 1.0, g[:, 8:12], ALU.is_equal, ALU.mult, [t], "v_g")
        t = tt(zs[:, sl, 0:32].rearrange("p (e r) -> p e r", e=4), ps[:, 6, 0:32].rearrange("p (e r) -> p e r", e=4),
               g[:, 16:20].unsqueeze(2).broadcast_to([128, 4, 8]), ALU.mult, [t, t_zz] + fr(("zs", sl)), "v_z")
        free["b6"] = [t]
        free[("g", sl)] = [t]
        tok_z[i] = t

    def z_trans(i):
        sl = i % 2
        t = transpose(ps[:, 7, 0:128], zs[:, sl, :], identf[:, :], [tok_z[i]] + fr("b7"), "t_z")
        free[("zs", sl)] = [t]
        w = fr(("zt", sl))
        th = copy_hi(zth[:, sl, :], ps[:, 7, 0:128], [t] + w, "a_z")
        tl = sub_lo(DV, ztl[:, sl, :], ps[:, 7, 0:128], zth[:, sl, :], [th] + w, "v_zl")
        free["b7"] = [tl]
        tok_zt[i] = [th, tl]

    def main3(i, k, nh, bk):
        sl = i % 2
        mm3(bank(bk), h4h[:, sl, k, :], h4l[:, sl, k, :], uph[:, k, nh * 512:nh * 512 + 512],
            upl[:, k, nh * 512:nh * 512 + 512], k == 0, False,
            tok_up[k] + tok_h4[i] + (fr(("b", bk)) if k == 0 else []))

    tok_out = []

    def end3(i, bks):
        sl = i % 2
        for nh in range(2):
            t = mm3(bank(bks[nh]), zth[:, sl, :], ztl[:, sl, :], lbh[:, nh * 512:nh * 512 + 512],
                    lbl[:, nh * 512:nh * 512 + 512], False, True, tok_zt[i] + tok_lb, "t_l3")
            t2 = tt(y[:, sl, nh * 512:nh * 512 + 512], bank(bks[nh]), x3[:, i % 3, nh * 512:nh * 512 + 512], ALU.add,
                    [t, t_x3[i]] + fr(("y", sl)), "v_y")
            free[("b", bks[nh])] = [t2]
        free[("h4t", sl)] = free[("zt", sl)] = [t]
        free[("x3", i % 3)] = [t2]
        td = dma(out[i], y[:, sl, :], [t2], f"d_y{sl}")
        free[("y", sl)] = [td]
        tok_out.append(td)

    for k in range(4):
        load_up(k)
    load_x3(2)
    t0 = norm3(0)
    trans3(0, t0)
    th = copy_hi(lbh[:, :], lbr[:, :], [t_lb], "a_lb")
    tok_lb = [th, sub_lo(PO, lbl[:, :], lbr[:, :], lbh[:, :], [th], "p_lb")]
    t1 = norm3(1)
    trans3(1, t1)
    for k in range(4, 8):
        load_up(k)
    gate(0)
    gate(1)
    for k in range(8):
        for i in range(2):
            for nh in range(2):
                main3(i, k, nh, 2 * i + nh)
        if k == 2:
            z_trans(0)
        if k == 4:
            z_trans(1)
    t2 = norm3(2)
    end3(0, [0, 1])
    load_x3(3)
    trans3(2, t2)
    end3(1, [2, 3])
    load_x3(4)
    gate(2)
    for i in range(2, 8):
        bks = [2 * (i % 2), 2 * (i % 2) + 1]
        for k in range(8):
            main3(i, k, 0, bks[0])
        z_trans(i)
        if i + 1 < 8:
            t = norm3(i + 1)
            trans3(i + 1, t)
        for k in range(8):
            main3(i, k, 1, bks[1])
        if i + 1 < 8:
            gate(i + 1)
        end3(i, bks)
        if i + 3 < 8:
            load_x3(i + 3)
    three.close()
    Q.op(SP, lambda e: None, tok_out)

    block = ctx.enter_context(nc.Block())

    @block.sync
    def _(e):
        Q.emit(SP, e)

    @block.tensor
    def _(e):
        Q.emit(PE, e)

    @block.vector
    def _(e):
        Q.emit(DV, e)

    @block.scalar
    def _(e):
        Q.emit(AC, e)

    @block.gpsimd
    def _(e):
        Q.emit(PO, e)


def kernel(**inp):
    import ml_dtypes
    import numpy as np
    import concourse.bacc as bacc
    from concourse.bass_utils import run_bass_kernel_spmd as run

    def c(a):
        return np.ascontiguousarray(a)

    f = {k: np.asarray(v) for k, v in inp.items()}
    ctx = f["ctx_4096"]

    def slices(w, n):
        return c(w.reshape(8, 128, n, 128).transpose(2, 1, 0, 3).reshape(n, 128, 1024))

    def rows(w, m):
        return c(w.reshape(8, 128, m).transpose(1, 0, 2).reshape(128, 8 * m))

    inv = (np.float32(1.0) / (np.float64(10000.0) ** (np.arange(0, 128, 2, dtype=np.float32) / np.float32(128)))
           .astype(np.float32)).astype(np.float32)
    ang = (np.arange(1024, dtype=np.float32)[None, :] * inv[:, None]).astype(np.float32)
    cos, sin = np.cos(ang.astype(np.float64)), np.sin(ang.astype(np.float64))
    root = float(np.sqrt(np.float32(128.0)))
    cosk = np.concatenate([cos, cos], 0).astype(np.float32)
    sink = np.concatenate([sin, -sin], 0).astype(np.float32)
    cosq = (np.concatenate([cos, cos], 0)[:, :512] / root).astype(np.float32)
    sinq = (np.concatenate([sin, -sin], 0)[:, :512] / root).astype(np.float32)
    scal = np.concatenate([f[n].reshape(1) for n in
                           ("L0_xattn_x1_scale", "L0_xattn_x1_zp", "L0_xattn_x2_scale", "L0_xattn_x2_zp")])
    onehot = np.zeros((128, 8), np.float32)
    onehot[np.arange(128), np.arange(128) // 16] = 1
    rb = np.concatenate([np.tile(f["L0_ffn_router_b"][None, :], (128, 1)), onehot], 1)
    eb = np.concatenate([np.tile(f["L1_ffn_expert_bias"][None, :], (128, 1)), np.ones((128, 4), np.float32)], 1)
    arrays = {
        "identf": np.eye(128, dtype=np.float32),
        "identb": np.eye(128).astype(ml_dtypes.bfloat16),
        "onesb": np.ones((128, 128), ml_dtypes.bfloat16),
        "x": f["x"].reshape(8, 128, 1024),
        "ctx": ctx.reshape(2, 8, 128, 1024),
        "ctxT": ctx.transpose(0, 2, 1).reshape(2, 8, 128, 1024),
        "mask": f["mask_BxSxS2_ff0"].reshape(8, 128, 1024),
        "scal": np.tile(scal[None, :], (128, 1)),
        "cosk": cosk, "sink": sink, "cosq": cosq, "sinq": sinq,
        "wk": slices(f["L1_xattn_wk"], 8), "wv": slices(f["L1_xattn_wv"], 8), "wq": slices(f["L1_xattn_wq"], 32),
        "wo": f["L1_xattn_wo"].reshape(32, 128, 1024),
        "W": f["L0_ffn_W"].T.reshape(8, 128, 1024),
        "bias": np.tile(f["L0_ffn_b"][None, :], (128, 1)),
        "loraA": rows(f["L0_ffn_A"].reshape(128, 1024).T, 128),
        "loraB": f["L0_ffn_B"].transpose(0, 2, 1).reshape(128, 1024),
        "rw": rows(f["L0_ffn_router_W"].T, 8),
        "rb": rb, "eb": eb,
        "up": f["L1_ffn_W_up"].T.reshape(8, 128, 1024),
        "ag": rows(np.concatenate([f["L1_ffn_lora_A"].reshape(32, 1024).T, f["L1_ffn_gate_w"].T], 1), 36),
        "lb": f["L1_ffn_lora_B"].transpose(0, 2, 1).reshape(32, 1024),
    }
    nc = bacc.Bacc("TRN2", target_bir_lowering=False, num_devices=1)
    arrays = {"in_" + k: c(v) for k, v in arrays.items()}
    aps = {k[3:]: nc.dram_tensor(k, v.shape, mybir.dt.from_np(v.dtype), kind="ExternalInput").ap()
           for k, v in arrays.items()}
    o = nc.dram_tensor("out_0", (8, 128, 1024), F32, kind="ExternalOutput").ap()
    build(nc, aps, o)
    r = run(nc, [arrays], core_ids=[0])
    return r.results[0]["out_0"].reshape(2, 512, 1024)
```

```python
from contextlib import ExitStack

import concourse.bass as bass
from concourse import mybir

F32 = mybir.dt.float32
F32R = mybir.dt.float32r
BF16 = mybir.dt.bfloat16
ALU = mybir.AluOpType
ACT = mybir.ActivationFunctionType
AX = mybir.AxisListType.X

MAGIC = 12582912.0
EPS = 1e-5
LOWEST = -3.4028234663852886e38
SP, PE, DV, AC, PO = "sync", "tensor", "vector", "scalar", "gpsimd"


class Queues:

    def __init__(self, nc, ctx):
        self.nc, self.ctx = nc, ctx
        self.q = {e: [] for e in (SP, PE, DV, AC, PO)}
        self.sems, self.count = {}, {}

    def op(self, eng, fn, w=(), s=None, inc=1):
        for name, value in w:
            self.q[eng].append((name, value, None))
        if s is None:
            self.q[eng].append((None, 0, fn))
            return None
        if s not in self.sems:
            self.sems[s] = self.ctx.enter_context(self.nc.semaphore(s))
            self.count[s] = 0
        self.count[s] += inc
        sem = self.sems[s]
        self.q[eng].append((None, 0, lambda e: fn(e).then_inc(sem, inc)))
        return (s, self.count[s])

    def dma(self, dst, src, w=(), s=None, eng=SP):
        return self.op(eng, lambda e: e.dma_start(dst, src), w, s, 16)

    def emit(self, eng, e):
        seen = {}
        for name, value, fn in self.q[eng]:
            if fn is not None:
                fn(e)
            elif seen.get(name, 0) < value:
                seen[name] = value
                e.wait_ge(self.sems[name], value)


def fl(ap):
    return ap.rearrange("p a b -> p (a b)")


def f32(ap):
    return ap.bitcast(F32)


def build(nc, A, out):
    with ExitStack() as ctx:
        build_in(nc, ctx, A, out)


def build_in(nc, ctx, A, out):
    Q = Queues(nc, ctx)
    op, dma = Q.op, Q.dma

    def alloc(stack, name, shape, dt=F32):
        return stack.enter_context(nc.sbuf_tensor(name, shape, dt))

    ps = ctx.enter_context(nc.psum_tensor("ps", [128, 8, 512], F32))
    k_d = nc.dram_tensor("k_scratch", [16, 128, 2, 1024], F32, kind="Internal").ap()
    v_d = nc.dram_tensor("v_scratch", [16, 128, 2, 1024], F32, kind="Internal").ap()
    h_d = nc.dram_tensor("h_scratch", [2, 128, 8, 2, 512], F32, kind="Internal").ap()
    x2_d = nc.dram_tensor("x2_scratch", [8, 128, 1024], F32, kind="Internal").ap()
    x3_d = nc.dram_tensor("x3_scratch", [8, 128, 1024], F32, kind="Internal").ap()

    def bank(b):
        return ps[:, b, :]

    def pair(b):
        return fl(ps[:, b:b + 2, :])

    def copy_hi(dst, src, w, s):
        return op(AC, lambda e: e.copy(dst, src), w, s)

    def sub_lo(eng, dst, src, hi, w, s):
        return op(eng, lambda e: e.tensor_tensor(dst, src, f32(hi), ALU.subtract), w, s)

    def tt(dst, a, b, o, w, s, eng=DV):
        return op(eng, lambda e: e.tensor_tensor(dst, a, b, o), w, s)

    def tsc(dst, a, s1, s2, o1, o2, w, s):
        if o2 is None:
            return op(DV, lambda e: e.tensor_scalar(dst, a, s1, None, o1), w, s)
        return op(DV, lambda e: e.tensor_scalar(dst, a, s1, s2, o1, o2), w, s)

    def stt(dst, a, sc, b, o1, o2, w, s):
        return op(DV, lambda e: e.scalar_tensor_tensor(out=dst, in0=a, scalar=sc, in1=b, op0=o1, op1=o2), w, s)

    def mm(dst, l, r, start, stop, w=(), s=None):
        return op(PE, lambda e: e.matmul(dst, l, r, start=start, stop=stop), w, s)

    def mm3(dst, lh, ll, rh, rl, start, stop, w=(), s=None):
        mm(dst, ll, rh, start, False, w)
        mm(dst, lh, rl, False, False)
        return mm(dst, lh, rh, False, stop, (), s)

    def transpose(dst, src, ident, w=(), s=None):
        return op(PE, lambda e: e.transpose(dst, src, ident), w, s)

    identf = alloc(ctx, "identf", [128, 128])
    sm = alloc(ctx, "sm", [128, 4, 20])
    scal = alloc(ctx, "scal", [128, 16])
    small = alloc(ctx, "small", [128, 128])

    ln_n = [0]

    def layernorm(x, dst, w, wdst, s):
        c = sm[:, ln_n[0] % 4, :]
        ln_n[0] += 1
        op(DV, lambda e: e.bn_stats(c[:, 0:6], x[:, 0:512]), w)
        t = op(DV, lambda e: e.bn_stats(c[:, 6:12], x[:, 512:1024]), (), "v_ln")
        t = op(DV, lambda e: e.bn_aggr(c[:, 12:14], c[:, 0:12]), [t], "v_ln")
        t = tsc(c[:, 14:15], c[:, 13:14], EPS, None, ALU.add, None, [t], "v_ln")
        t = op(AC, lambda e: e.activation(c[:, 15:16], c[:, 14:15], ACT.Sqrt), [t], "a_sqrt")
        t = op(DV, lambda e: e.reciprocal(c[:, 16:17], c[:, 15:16]), [t], "v_ln")
        t = tsc(c[:, 17:18], c[:, 16:17], c[:, 16:17], c[:, 14:15], ALU.mult, ALU.mult, [t], "v_ln")
        t = tsc(c[:, 18:19], c[:, 17:18], -0.5, 1.5, ALU.mult, ALU.add, [t], "v_ln")
        t = tsc(c[:, 19:20], c[:, 18:19], c[:, 16:17], None, ALU.mult, None, [t], "v_ln")
        return tsc(dst, x, c[:, 12:13], c[:, 19:20], ALU.subtract, ALU.mult, [t] + wdst, s)

    def rope(src, cos, sin, u, t, w, wu, s):
        tt(u, src, cos, ALU.mult, w + wu, None)
        tt(t[0:64], src[64:128], sin[64:128], ALU.mult, (), None)
        return tt(t[64:128], src[0:64], sin[0:64], ALU.mult, (), s)

    NR = 3
    one = ExitStack()
    x_lo = alloc(one, "x_lo", [128, 4, 1024])
    raw = alloc(one, "raw", [128, NR, 1024])
    spare = alloc(one, "spare", [128, 2, 1024], F32R)
    x_hi = alloc(one, "x_hi", [128, 4, 1024])
    slots = alloc(one, "slots", [128, 8, 2, 1024], F32R)
    wh = alloc(one, "wh", [128, 2, 1024], F32R)
    wl = alloc(one, "wl", [128, 2, 1024], F32R)
    cosk = alloc(one, "cosk", [128, 1024])
    sink = alloc(one, "sink", [128, 1024])
    u_sb = alloc(one, "u_sb", [128, 2, 512])
    t_sb = alloc(one, "t_sb", [128, 512])
    khl = alloc(one, "khl", [128, 2, 2, 512], F32R)
    ctab = alloc(one, "ctab", [128, 1024])
    tmp = alloc(one, "tmp", [128, 3, 1024])
    ts_sb = alloc(one, "ts_sb", [128, 2, 512], F32R)
    l0 = ExitStack()
    identb = alloc(l0, "identb", [128, 128], BF16)
    onesb = alloc(l0, "onesb", [128, 128], BF16)
    bq = alloc(l0, "bq", [128, 8, 1024], BF16)
    a1T = alloc(l0, "a1T", [128, 8, 512], BF16)
    a_sb = alloc(l0, "a_sb", [128, 2, 1024], BF16)
    l0.close()
    h2 = ExitStack()
    h2h = alloc(h2, "h2h", [128, 8, 512], F32R)
    h2l = alloc(h2, "h2l", [128, 8, 512], F32R)
    h2.close()
    one.close()
    two = ExitStack()
    hTa = alloc(two, "hTa", [128, 4, 2, 512], F32R)
    wqh = alloc(two, "wqh", [128, 3, 512], F32R)
    wql = alloc(two, "wql", [128, 3, 512], F32R)
    araw = alloc(two, "araw", [128, 4, 512])
    hTb = alloc(two, "hTb", [128, 4, 2, 512], F32R)
    ksb = alloc(two, "ksb", [128, 2, 2, 1024], F32R)
    mask = alloc(two, "mask", [128, 4, 1024])
    cosq = alloc(two, "cosq", [128, 512])
    sinq = alloc(two, "sinq", [128, 512])
    psb = alloc(two, "psb", [128, 3, 1024])
    qsb = alloc(two, "qsb", [128, 2, 2, 512], F32R)
    pth = alloc(two, "pth", [128, 8, 512], F32R)
    ptl = alloc(two, "ptl", [128, 8, 512], F32R)
    vsb = alloc(two, "vsb", [128, 2, 1024], F32R)
    osb = alloc(two, "osb", [128, 2, 2, 2, 512], F32R)
    woh = alloc(two, "woh", [128, 2, 2, 512], F32R)
    wol = alloc(two, "wol", [128, 2, 2, 512], F32R)
    ua = alloc(two, "ua", [128, 512])
    ta = alloc(two, "ta", [128, 512])
    rb = alloc(two, "rb", [128, 512])
    xa = alloc(two, "xa", [128, 4, 1024])
    st = alloc(two, "st", [128, 4, 16])
    two.close()
    three = ExitStack()
    upa = alloc(three, "upa", [128, 2, 2, 1024], F32R)
    upb = alloc(three, "upb", [128, 1, 2, 1024], F32R)
    ag_raw = alloc(three, "ag_raw", [128, 288])
    agh = alloc(three, "agh", [128, 8, 36], F32R)
    agl = alloc(three, "agl", [128, 8, 36], F32R)
    alloc(three, "pad0", [128, 160])
    raw3 = alloc(three, "raw3", [128, 2, 1024])
    upc = alloc(three, "upc", [128, 2, 2, 1024], F32R)
    upd = alloc(three, "upd", [128, 1, 2, 1024], F32R)
    h4 = alloc(three, "h4", [128, 2, 1024])
    x3 = alloc(three, "x3", [128, 3, 1024])
    lbr = alloc(three, "lbr", [128, 1024])
    h4h = alloc(three, "h4h", [128, 2, 8, 128], F32R)
    h4l = alloc(three, "h4l", [128, 2, 8, 128], F32R)
    alloc(three, "pad1", [128, 2048])
    upe = alloc(three, "upe", [128, 2, 2, 1024], F32R)
    lbh = alloc(three, "lbh", [128, 1024], F32R)
    lbl = alloc(three, "lbl", [128, 1024], F32R)
    y = alloc(three, "y", [128, 2, 1024])
    zs = alloc(three, "zs", [128, 2, 128])
    zth = alloc(three, "zth", [128, 2, 128], F32R)
    ztl = alloc(three, "ztl", [128, 2, 128], F32R)
    g_sb = alloc(three, "g_sb", [128, 2, 32])
    eb = alloc(three, "eb", [128, 8])
    three.close()

    def x_tile(i):
        return x_lo[:, i, :] if i < 4 else x_hi[:, i - 4, :]

    def slot(i, hl):
        s = i % 9
        if s == 6:
            return spare[:, hl, :]
        return slots[:, s if s < 6 else s - 1, hl, :]

    free = {}

    def fr(key):
        return list(free.get(key, []))

    raws = [(r, []) for r in range(NR)]

    def load_split(src, hi, lo, w, eng=PO):
        r, wr = raws.pop(0)
        d = dma(raw[:, r, :], src, wr, f"d_raw{r}")
        h = copy_hi(hi, raw[:, r, :], [d] + w, "a_hi")
        l = sub_lo(eng, lo, raw[:, r, :], hi, [h] + w, "p_lo" if eng == PO else "v_lo")
        raws.append((r, [l]))
        return [h, l]

    tok_c = {}

    def load_c(i, eng=PO):
        src = A["ctxT"][i // 8, i % 8] if i < 16 else A["W"][i - 16]
        tok_c[i] = load_split(src, slot(i, 0), slot(i, 1), fr(("c", i % 9)), eng)

    units = [(b, g, kind) for b in range(2) for g in range(8) for kind in "kv"]
    tok_w = {}

    def load_w(n, eng=PO):
        if n < 32:
            b, g, kind = units[n]
            src = A["wk" if kind == "k" else "wv"][g]
        else:
            src = A["loraA"] if n == 32 else A["loraB"]
        tok_w[n] = load_split(src, wh[:, n % 2, :], wl[:, n % 2, :], fr(("w", n % 2)), eng)

    load_w(0)
    load_c(0, DV)
    load_w(1)
    for k in range(1, 8):
        load_c(k, DV if k % 2 else PO)
    t_cos = [dma(cosk[:, :], A["cosk"], (), "d_cosk"), dma(sink[:, :], A["sink"], (), "d_sink")]
    t_id = dma(identf[:, :], A["identf"], (), "d_identf")
    t_idb = [dma(identb[:, :], A["identb"], (), "d_identb"), dma(onesb[:, :], A["onesb"], (), "d_onesb")]
    t_sc = dma(scal[:, 0:4], A["scal"], (), "d_scal")
    t_x = {}
    for i in range(8):
        t_x[i] = [dma(x_tile(i), A["x"][i], (), f"d_x{i}")]

    tsc(scal[:, 6:7], scal[:, 1:2], -1.0, 128.0, ALU.mult, ALU.add, [t_sc], None)
    tsc(scal[:, 7:8], scal[:, 3:4], -1.0, 128.0, ALU.mult, ALU.add, (), None)
    op(DV, lambda e: e.reciprocal(scal[:, 4:5], scal[:, 0:1]))
    op(DV, lambda e: e.reciprocal(scal[:, 5:6], scal[:, 2:3]))
    t_s = tt(scal[:, 8:9], scal[:, 0:1], scal[:, 2:3], ALU.mult, (), "v_scal")
    t_s = tsc(scal[:, 9:10], scal[:, 6:7], scal[:, 7:8], 1024.0, ALU.mult, ALU.mult, [t_s], "v_scal")

    kv_n = [0]
    tok_kd, tok_vd = {}, {}
    late = []

    def kv_products(group):
        banks = [(kv_n[0] + j) % 4 for j in range(len(group))]
        last = {}
        for k in range(8):
            for j, (n, half) in enumerate(group):
                b, bk = units[n][0], banks[j]
                c = b * 8 + k
                rh = slot(c, 0)[:, half * 512:half * 512 + 512]
                rl = slot(c, 1)[:, half * 512:half * 512 + 512]
                lh, ll = wh[:, n % 2, k * 128:k * 128 + 128], wl[:, n % 2, k * 128:k * 128 + 128]
                end = n % 16 == 15 and half == 1
                last[j] = mm3(bank(bk), lh, ll, rh, rl, k == 0, k == 7,
                              tok_w[n] + tok_c[c] + (fr(("b", bk)) if k == 0 else []),
                              "t_kv" if k == 7 or end else None)
                if end:
                    free[("c", c % 9)] = [last[j]]
        for j, (n, half) in enumerate(group):
            free[("w", n % 2)] = [last[j]]
        return [(n, half, banks[j], last[j]) for j, (n, half) in enumerate(group)]

    stores = []

    def store(dst, o, w, toks):
        def issue():
            td = dma(dst, f32(khl[:, o, :, :]), w, f"d_khl{o}")
            free[("khl", o)] = [td]
            toks.append(td)
        stores.append(issue)

    def issue_stores():
        while stores:
            stores.pop(0)()

    def kv_store(n, half, bk, t):
        b, g, kind = units[n]
        o = kv_n[0] % 2
        kv_n[0] += 1
        u = u_sb[:, o, :]
        if kind == "k":
            cs = slice(half * 512, half * 512 + 512)
            tr = rope(bank(bk), cosk[:, cs], sink[:, cs], u, t_sb[:, :], [t] + t_cos + fr("t"), fr(("u", o)), "v_kr")
            free[("b", bk)] = [tr]
            tu = tt(u, u, t_sb[:, :], ALU.add, [tr], "p_ku", eng=PO)
            free["t"] = [tu]
            th = copy_hi(khl[:, o, 0, :], u, [tu] + fr(("khl", o)), "a_khi")
            tl = sub_lo(PO, khl[:, o, 1, :], u, khl[:, o, 0, :], [th] + fr(("khl", o)), "p_klo")
            free[("u", o)] = [tl]
            store(k_d[b * 8 + g, :, :, cs], o, [th, tl], tok_kd.setdefault(b * 8 + g, []))
            return
        tu = op(AC, lambda e: e.copy(u, bank(bk)), [t] + fr(("u", o)), "a_vt")
        free[("b", bk)] = [tu]

        def finish():
            for j in range(4):
                t2 = transpose(ps[:, 6, j * 128:j * 128 + 128], u[:, j * 128:j * 128 + 128], identf[:, :],
                               [tu, t_id] + fr(("b", 6)), "t_vtr" if j == 3 else None)
            free[("u", o)] = [t2]
            th = copy_hi(khl[:, o, 0, :], bank(6), [t2] + fr(("khl", o)), "a_khi")
            tl = sub_lo(DV, khl[:, o, 1, :], bank(6), khl[:, o, 0, :], [th] + fr(("khl", o)), "v_klo")
            free[("b", 6)] = [tl]
            store(v_d[b * 8 + g, :, :, half * 512:half * 512 + 512], o, [th, tl], tok_vd.setdefault(b * 8 + g, []))

        late.append(finish)

    temps = [(tmp[:, k, :], []) for k in range(3)]

    def take():
        return temps.pop(0)

    def give(t, toks):
        temps.append((t, toks))

    R = small[:, 0:8]

    def quantise(q, src, rs, z, dst, w, wd, s):
        t = tsc(q, src, scal[:, rs:rs + 1], scal[:, z:z + 1], ALU.mult, ALU.add, w, "v_q")
        t2 = tsc(q, q, MAGIC, MAGIC, ALU.add, ALU.max, [t], "v_q")
        t3 = tsc(dst, q, MAGIC + 255.0, -(MAGIC + 128.0), ALU.min, ALU.add, [t2] + wd, s)
        return t, t3

    tok_a1T, tok_bq = [], {}
    n_a = [0]

    def background_x(b):
        pend = []
        for i in range(4):
            tile = b * 4 + i
            h, wh_ = take()
            th = layernorm(x_tile(tile), h, t_x[tile], wh_, "v_h")
            yield
            while pend:
                pend.pop(0)()
            a = n_a[0] % 2
            n_a[0] += 1
            av = a_sb[:, a, :]
            _, ta_ = quantise(h, h, 4, 1, av, [th, t_s], fr(("a", a)), "v_a")
            give(h, [ta_])
            t = op(AC, lambda e, av=av, tile=tile: e.activation(av, av, ACT.Copy, accum_out=R[:, tile:tile + 1]),
                   [ta_], "a_rs")
            tsc(R[:, tile:tile + 1], R[:, tile:tile + 1], scal[:, 7:8], None, ALU.mult, None, [t], "v_rs")

            def turn(i=i, a=a, t=t):
                pb = bank(7).bitcast(BF16)
                for k8 in range(8):
                    t2 = transpose(pb[:, k8 * 128:k8 * 128 + 128], a_sb[:, a, k8 * 128:k8 * 128 + 128], identb[:, :],
                                   [t] + t_idb + fr(("b", 7)), "t_atr" if k8 == 7 else None)
                free[("a", a)] = [t2]
                t2 = op(AC, lambda e: e.copy(a1T[:, :, i * 128:i * 128 + 128],
                                             pb.rearrange("p (k t) -> p k t", k=8)),
                        [t2] + fr("a1T"), "a_a1T")
                free[("b", 7)] = [t2]
                tok_a1T.append(t2)

            pend.append(turn)
            yield
        while pend:
            pend.pop(0)()

    def background_c(b):
        def load(k):
            r, wr = raws.pop(0)
            return r, dma(raw[:, r, :], A["ctx"][b, k], wr, f"d_raw{r}")

        ahead = load(0)
        yield
        for k in range(8):
            r, d = ahead
            if k < 7:
                ahead = load(k + 1)
            _, tq = quantise(raw[:, r, :], raw[:, r, :], 5, 3, bq[:, k, :], [d, t_s], fr("bq"), "v_bq")
            raws.append((r, [tq]))
            tok_bq[k] = tq
            yield

    def l0_product(b):
        w = list(tok_a1T) + list(tok_bq.values()) + t_idb
        for nh in range(2):
            for k in range(8):
                t = mm(bank(4 + nh), onesb[:, :], bq[:, k, nh * 512:nh * 512 + 512], k == 0, k == 7,
                       w + fr(("b", 4 + nh)), "t_l0" if k == 7 else None)
            t_c = tsc(ctab[:, nh * 512:nh * 512 + 512], bank(4 + nh), scal[:, 6:7], scal[:, 9:10], ALU.mult, ALU.add,
                      [t], "v_ctab")
            free[("b", 4 + nh)] = [t_c]
        for n in range(8):
            i, nh = n // 2, n % 2
            tile, bk = b * 4 + i, 4 + n % 2
            for k in range(8):
                t = mm(bank(bk), a1T[:, k, i * 128:i * 128 + 128], bq[:, k, nh * 512:nh * 512 + 512],
                       k == 0, k == 7, fr(("b", bk)), "t_l0" if k == 7 else None)
            q, wq_ = take()
            xs = x_tile(tile)[:, nh * 512:nh * 512 + 512]
            t2 = stt(q[:, 0:512], bank(bk), R[:, tile:tile + 1], ctab[:, nh * 512:nh * 512 + 512], ALU.add, ALU.add,
                     [t, t_c] + wq_, "v_l0")
            free[("b", bk)] = [t2]
            t3 = stt(xs, q[:, 0:512], scal[:, 8:9], xs, ALU.mult, ALU.add, [t2], "v_l0")
            give(q, [t3])
            t_x[tile] = [t3]
        free["bq"] = free["a1T"] = [t]
        tok_a1T.clear()
        free["ctab"] = [t2]
        return t

    def finish_late():
        while late:
            late.pop(0)()

    def run_kv(ns, bx, bc=iter(())):
        ns = list(ns)
        if ns[0] % 16 == 0:
            groups = [[(ns[0], 0), (ns[0], 1), (ns[1], 0), (ns[1], 1)]]
            ns = ns[2:]
        else:
            groups = []
        groups += [[(n, half)] for n in ns for half in range(2)]
        for group in groups:
            if len(group) == 1 and group[0][1] == 0 and group[0][0] + 1 not in tok_w:
                load_w(group[0][0] + 1)
            issue_stores()
            done = kv_products(group)
            if len(group) > 1:
                load_w(group[-1][0] + 1, DV)
            several = len(late) > 1
            finish_late()
            if several:
                issue_stores()
            for u in done:
                if len(done) > 1:
                    issue_stores()
                kv_store(*u)
                next(bc if units[u[0]][2] == "k" else bx, None)
        for rest in (bc, bx):
            for _ in rest:
                pass

    run_kv(range(0, 16), background_x(0), background_c(0))
    finish_late()
    load_w(17)
    for k in range(8):
        load_c(8 + k)
    l0_product(0)
    run_kv(range(16, 24), background_x(1), background_c(1))
    finish_late()
    t_l0 = l0_product(1)
    w_h2 = [t_l0]
    t_bias = dma(ctab[:, :], A["bias"], fr("ctab"), "d_bias")
    t_rt = [dma(small[:, 64:128], A["rw"], (), "d_rw"), dma(small[:, 40:56], A["rb"], (), "d_rb")]
    tok_h2, tok_ts = {}, {}

    def ffn_norm(tile):
        h, w = take()
        t = layernorm(x_tile(tile), h, t_x[tile], w, "v_h")
        t_x[tile] = [tt(x_tile(tile), x_tile(tile), ctab[:, :], ALU.add, [t, t_bias], "p_xb", eng=PO)]
        return h, t

    def tile_transposes(h, t):
        for j in range(8):
            t2 = transpose(ps[:, 4 + j // 4, (j % 4) * 128:(j % 4) * 128 + 128], h[:, j * 128:j * 128 + 128],
                           identf[:, :], [t, t_id] + (fr(("b", 4)) + fr(("b", 5)) if j == 0 else []),
                           "t_htr" if j == 7 else None)
        give(h, [t2])
        return t2

    def ffn_transposes(tile, h, t):
        i = tile % 4
        t2 = tile_transposes(h, t)
        dst = h2h[:, :, i * 128:i * 128 + 128]
        src = pair(4).rearrange("p (k t) -> p k t", k=8)
        w = w_h2 + fr(("h2", i))
        th = copy_hi(dst, src, [t2] + w, "a_h2")
        tl = sub_lo(DV, h2l[:, :, i * 128:i * 128 + 128], src, dst, [th] + w, "v_h2")
        free[("b", 4)] = free[("b", 5)] = [tl]
        tok_h2[i] = [th, tl]

    def router(b):
        w = [x for v in tok_h2.values() for x in v]
        op(DV, lambda e: e.tensor_reduce(small[:, 8:16], f32(h2h[:, :, 179:511]), AX, ALU.add), w)
        t = op(DV, lambda e: e.tensor_reduce(small[:, 16:24], f32(h2l[:, :, 179:511]), AX, ALU.add), (), "v_rt")
        t = tt(small[:, 8:16], small[:, 8:16], small[:, 16:24], ALU.add, [t], "v_rt")
        qbc, wq_ = take()
        t_q = op(DV, lambda e: e.tensor_copy(qbc.rearrange("p (k m) -> p k m", k=8),
                                             small[:, 8:16].unsqueeze(2).broadcast_to([128, 8, 128])),
                 [t] + wq_, "v_rt")

        def end():
            for k in range(8):
                t2 = mm(ps[:, 6, 0:8], qbc[:, k * 128:k * 128 + 128], small[:, 64 + k * 8:72 + k * 8], k == 0, k == 7,
                        [t_q] + t_rt + fr(("b", 6)), "t_rt" if k == 7 else None)
            give(qbc, [t2])
            t = stt(small[:, 16:24], ps[:, 6, 0:8], 1.0 / 332.0, small[:, 40:48], ALU.mult, ALU.add, [t2], "v_rt")
            free[("b", 6)] = [t]
            t = op(DV, lambda e: e.reduce_max(small[:, 32:33], small[:, 16:24], AX), [t], "v_rt")
            t = tsc(small[:, 33:34], small[:, 32:33], -1.0, None, ALU.mult, None, [t], "v_rt")
            t = op(AC, lambda e: e.activation(small[:, 24:32], small[:, 16:24], ACT.Exp, bias=small[:, 33:34],
                                              accum_out=small[:, 34:35]), [t], "a_rt")
            t = op(DV, lambda e: e.reciprocal(small[:, 35:36], small[:, 34:35]), [t], "v_rt")
            t = op(DV, lambda e: e.tensor_tensor_reduce(out=small[:, 56:64], in0=small[:, 24:32],
                                                        in1=small[:, 48:56], scale=2.0, scalar=0.0, op0=ALU.mult,
                                                        op1=ALU.add, accum_out=small[:, 36:37]), [t], "v_rt")
            return tsc(small[:, 37 + b:38 + b], small[:, 36:37], small[:, 35:36], None, ALU.mult, None, [t], "v_rt")

        return end

    held, tok_r = {}, {}

    def background_ffn():
        held[0] = ffn_norm(0)
        yield
        for i in range(1, 4):
            held[i] = ffn_norm(i)
            ffn_transposes(i - 1, *held[i - 1])
            yield
        ffn_transposes(3, *held[3])
        yield
        end = router(0)
        yield
        tok_r[0] = end()
        held[4] = ffn_norm(4)
        yield
        held[5] = ffn_norm(5)
        yield

    steps = background_ffn()
    run_kv(range(24, 31), steps, steps)
    load_w(32)
    load_c(16)
    for half in range(2):
        issue_stores()
        done = kv_products([(31, half)])
        finish_late()
        kv_store(*done[0])
    t_kv_end = done[0][3]
    temps.append((cosk[:, :], [("v_kr", Q.count["v_kr"])]))
    for i in range(17, 19):
        load_c(i)
    load_w(33)

    def lora_t(b):
        for k in range(8):
            t = mm3(bank(7), wh[:, 0, k * 128:k * 128 + 128], wl[:, 0, k * 128:k * 128 + 128], h2h[:, k, :],
                    h2l[:, k, :], k == 0, k == 7,
                    tok_w[32] + [x for v in tok_h2.values() for x in v] + (fr(("b", 7)) if k == 0 else []),
                    "t_lt" if k == 7 else None)
        return t

    def lora_scale(b, t):
        u = u_sb[:, 0, :]
        t2 = tsc(u, bank(7), small[:, 37 + b:38 + b], None, ALU.mult, None, [t, tok_r[b]] + fr(("u", 0)), "v_ts")
        free[("b", 7)] = [t2]
        w = fr("ts")
        th = copy_hi(ts_sb[:, 0, :], u, [t2] + w, "a_ts")
        tl = sub_lo(DV, ts_sb[:, 1, :], u, ts_sb[:, 0, :], [th] + w, "v_tl")
        free[("u", 0)] = [tl]
        tok_ts[b] = [th, tl]

    tok_x2, tok_hd = {}, {}

    def ffn_main(i, k, nh, bk):
        return mm3(bank(bk), h2h[:, k, i * 128:i * 128 + 128], h2l[:, k, i * 128:i * 128 + 128],
                   slot(16 + k, 0)[:, nh * 512:nh * 512 + 512], slot(16 + k, 1)[:, nh * 512:nh * 512 + 512],
                   k == 0, False, tok_c[16 + k] + tok_h2[i] + (fr(("b", bk)) if k == 0 else []),
                   "t_fm" if k == 7 else None)

    def ffn_half(i, nh, bk):
        for k in range(8):
            t = ffn_main(i, k, nh, bk)
        if nh:
            free[("h2", i)] = [t]

    def ffn_end(b, i, bks):
        tile = b * 4 + i
        x = x_tile(tile)
        for nh in range(2):
            t = mm3(bank(bks[nh]), ts_sb[:, 0, i * 128:i * 128 + 128], ts_sb[:, 1, i * 128:i * 128 + 128],
                    wh[:, 1, nh * 512:nh * 512 + 512], wl[:, 1, nh * 512:nh * 512 + 512], False, True,
                    tok_w[33] + tok_ts[b], "t_fl")
            xs = x[:, nh * 512:nh * 512 + 512]
            t2 = tt(xs, bank(bks[nh]), xs, ALU.add, [t] + t_x[tile], "v_x2")
            free[("b", bks[nh])] = [t2]
        free["ts"] = [t]
        tok_x2[tile] = dma(x2_d[tile], x, [t2], f"d_x{tile}")
        h, w = take()
        t = layernorm(x, h, [t2], w, "v_h")
        held[("h3", tile)] = (h, t)
        return t

    def h3_out(tile):
        b, i = tile // 4, tile % 4
        t2 = tile_transposes(*held[("h3", tile)])
        for j in range(2):
            th = copy_hi(khl[:, j, 0, :], bank(4 + j), [t2] + fr(("khl", j)), "a_khi")
            tl = sub_lo(DV, khl[:, j, 1, :], bank(4 + j), khl[:, j, 0, :], [th], "v_klo")
            free[("b", 4 + j)] = [tl]
            for hl in range(2):
                td = dma(h_d[b, :, 4 * j:4 * j + 4, hl, i * 128:i * 128 + 128],
                         f32(khl[:, j, hl, :]).rearrange("p (k t) -> p k t", k=4), [tl, th], f"d_khl{j}")
            free[("khl", j)] = [td]
            tok_hd.setdefault(b, []).append(td)

    t = lora_t(0)
    issue_stores()
    finish_late()
    issue_stores()
    lora_scale(0, t)
    for i in range(19, 24):
        load_c(i)
    for k in range(8):
        for i in range(2):
            for nh in range(2):
                t = ffn_main(i, k, nh, 2 * i + nh)
    free[("h2", 0)] = free[("h2", 1)] = [t]
    ffn_end(0, 0, [0, 1])
    ffn_end(0, 1, [2, 3])
    ffn_half(2, 0, 0)
    h3_out(0)
    ffn_half(2, 1, 1)
    ffn_transposes(4, *held[4])
    h3_out(1)
    ffn_end(0, 2, [0, 1])
    held[6] = ffn_norm(6)
    ffn_half(3, 0, 2)
    ffn_transposes(5, *held[5])
    h3_out(2)
    ffn_half(3, 1, 3)
    ffn_transposes(6, *held[6])
    t_n3 = ffn_end(0, 3, [2, 3])
    held[7] = ffn_norm(7)
    ffn_half(0, 0, 0)
    h3_out(3)
    ffn_transposes(7, *held[7])
    ffn_half(0, 1, 1)
    end_r = router(1)
    t_lt = lora_t(1)
    ffn_half(1, 0, 2)
    tok_r[1] = end_r()
    lora_scale(1, t_lt)

    edge_x = [tok_x2[i] for i in range(4)] + [t_n3]
    edge_raw = [t for _, w in raws for t in w]
    tok_wq, tok_wo, tok_q, tok_h3 = {}, {}, {}, {}
    n_ar = [0]
    for r in range(4):
        free[("ar", r)] = [t_kv_end]
    for r in range(3):
        free[("wq", r)] = edge_raw

    def load_split2(src, hi, lo, w):
        r = n_ar[0] % 4
        n_ar[0] += 1
        d = dma(araw[:, r, :], src, fr(("ar", r)), f"d_ar{r}")
        h = copy_hi(hi, araw[:, r, :], [d] + w, "a_whi")
        l = sub_lo(PO, lo, araw[:, r, :], hi, [h] + w, "p_wlo")
        free[("ar", r)] = [l]
        return [h, l]

    def load_wq(n):
        if n >= 128:
            return
        head, half = (n // 2) % 32, n % 2
        sl = n % 3
        tok_wq[n] = load_split2(A["wq"][head, :, half * 512:half * 512 + 512], wqh[:, sl, :], wql[:, sl, :],
                                fr(("wq", sl)))

    def hT(k, hl):
        return hTa[:, k, hl, :] if k < 4 else hTb[:, k - 4, hl, :]

    def load_h(b, w, wt):
        dst = hTa[:, 2 * w:2 * w + 2, :, :] if w < 2 else hTb[:, 2 * w - 4:2 * w - 2, :, :]
        tok_h3[(b, w)] = dma(f32(dst), h_d[b, :, 2 * w:2 * w + 2, :, :], tok_hd[b] + wt, f"d_h{w}")

    ffn_end(1, 0, [0, 1])
    load_h(0, 0, edge_x)
    load_wq(0)
    ffn_half(1, 1, 3)
    h3_out(4)
    ffn_end(1, 1, [2, 3])
    load_h(0, 1, edge_x)
    load_wq(1)
    ffn_half(2, 0, 0)
    h3_out(5)
    ffn_half(2, 1, 1)
    ffn_end(1, 2, [0, 1])
    load_wq(2)
    ffn_half(3, 0, 2)
    h3_out(6)
    ffn_half(3, 1, 3)
    ffn_end(1, 3, [2, 3])

    edge_w = [("t_fl", Q.count["t_fl"])]
    edge_h = [("v_h", Q.count["v_h"]), ("p_xb", Q.count["p_xb"])] + [tok_x2[i] for i in range(4, 8)]

    def load_wo(q):
        j, nh = (q - 2) // 2, q % 2
        if q < 2 or j >= 32:
            return
        tok_wo[q] = []
        for i in range(2):
            head = (2 * j + i) % 32
            tok_wo[q] += load_split2(A["wo"][head, :, nh * 512:nh * 512 + 512], woh[:, nh, i, :], wol[:, nh, i, :],
                                     fr(("wo", nh)))

    tok_k, tok_v, tok_m, tok_xa = {}, {}, {}, {}

    def load_k(G):
        if G < 16:
            tok_k[G] = dma(f32(ksb[:, G % 2, :, :]), k_d[G], tok_kd[G] + fr(("k", G % 2)), f"d_k{G % 2}")

    def load_v(G):
        if G < 16:
            tok_v[G] = dma(f32(vsb[:, :, :]), v_d[G], tok_vd[G] + fr("v"), "d_v")

    def load_mask(b, i, w):
        tok_m[(b, i)] = dma(mask[:, i, :], A["mask"][b * 4 + i], w, f"d_m{i}")

    def q_part(H, k, bk=5):
        for k in (k, k + 1):
            n = 2 * H + k // 4
            sl = n % 3
            c = (k % 4) * 128
            t = mm3(bank(bk), wqh[:, sl, c:c + 128], wql[:, sl, c:c + 128], hT(k, 0), hT(k, 1),
                    k == 0, k == 7, tok_wq[n] + [tok_h3[(H // 32, k // 2)]] + (fr(("b", bk)) if k == 0 else []),
                    "t_q" if k % 2 else None)
        if k % 4 == 3:
            free[("wq", (2 * H + k // 4) % 3)] = [t]
        if H == 31:
            load_h(1, k // 2, [t])
        return t

    def q_end(H, t, bk=5):
        o = H % 2
        tr = rope(bank(bk), cosq[:, :], sinq[:, :], ua[:, :], ta[:, :], [t] + t_cq + fr("ta"), fr("ua"), "v_qr")
        free[("b", bk)] = [tr]
        tu = tt(ua[:, :], ua[:, :], ta[:, :], ALU.add, [tr], "p_qu", eng=PO)
        free["ta"] = [tu]
        w = fr(("q", o))
        th = copy_hi(qsb[:, o, 0, :], ua[:, :], [tu] + w, "a_qhi")
        tl = sub_lo(PO, qsb[:, o, 1, :], ua[:, :], qsb[:, o, 0, :], [th] + w, "p_qlo")
        free["ua"] = [tl]
        tok_q[H] = [th, tl]

    n_p = [0]
    tok_p, tok_pt = {}, {}

    def scores(H, i):
        b, G, o = H // 32, H // 4, H % 2
        for nh in range(2):
            t = mm3(bank(nh), qsb[:, o, 0, i * 128:i * 128 + 128], qsb[:, o, 1, i * 128:i * 128 + 128],
                    ksb[:, G % 2, 0, nh * 512:nh * 512 + 512], ksb[:, G % 2, 1, nh * 512:nh * 512 + 512], True, True,
                    tok_q[H] + [tok_k[G]] + fr("s_bank"), "t_s" if nh else None)
        if i == 3:
            free[("q", o)] = [t]
            if H % 4 == 3:
                free[("k", G % 2)] = [t]
        r = n_p[0] % 3
        n_p[0] += 1
        P = psb[:, r, :]
        c = st[:, H % 4, :]
        tm = op(DV, lambda e: e.tensor_tensor_reduce(out=P, in0=pair(0), in1=mask[:, i, :], scale=1.0,
                                                     scalar=LOWEST, op0=ALU.add, op1=ALU.max,
                                                     accum_out=c[:, i:i + 1]),
                [t, tok_m[(b, i)]] + fr(("p", r)), "v_max")
        free["s_bank"] = [tm]
        if H == 31:
            load_mask(1, i, [tm])
        tn = tsc(c[:, 4 + i:5 + i], c[:, i:i + 1], -1.0, None, ALU.mult, None, [tm], "v_nmax")
        te = op(AC, lambda e: e.activation(P, P, ACT.Exp, bias=c[:, 4 + i:5 + i], accum_out=c[:, 8 + i:9 + i]),
                [tn, tm], "a_exp")
        tok_p[(H, i)] = (r, te)

    turn_banks = [2, 3, 7]
    n_tb = [0]

    def next_turn_bank():
        bk = turn_banks[n_tb[0] % 3]
        n_tb[0] += 1
        return bk

    def p_turn(H, i, half):
        r, te = tok_p[(H, i)]
        bk = next_turn_bank()
        for k in range(4):
            c = (half * 4 + k) * 128
            t = transpose(ps[:, bk, k * 128:k * 128 + 128], psb[:, r, c:c + 128],
                          identf[:, :], [te] + fr(("tb", bk)), "t_p" if k == 3 else None)
        free[("p", r)] = [t]
        src = bank(bk).rearrange("p (k t) -> p k t", k=4)
        ks, qs = slice(half * 4, half * 4 + 4), slice(i * 128, i * 128 + 128)
        w = fr("pt")
        th = copy_hi(pth[:, ks, qs], src, [t] + w, "a_pt")
        tl = sub_lo(DV, ptl[:, ks, qs], src, pth[:, ks, qs], [th] + w, "v_pt")
        free[("tb", bk)] = [tl]
        tok_pt.setdefault(H, []).extend([th, tl])

    tok_rb, tok_ri = {}, {}

    def inverse(H):
        c = st[:, H % 4, :]
        tok_ri[H] = op(DV, lambda e: e.reciprocal(c[:, 12:16], c[:, 8:12]), [tok_p[(H, 3)][1]], "v_rinv")

    def inverse_rows(H):
        c = st[:, H % 4, :]
        bk = next_turn_bank()
        for i in range(4):
            t2 = transpose(ps[:, bk, i * 128:i * 128 + 128], c[:, 12 + i:13 + i].broadcast_to([128, 128]),
                           identf[:, :], [tok_ri[H]] + fr(("tb", bk)), "t_rb" if i == 3 else None)
        t3 = op(AC, lambda e: e.copy(rb[:, :], bank(bk)), [t2] + fr("rb"), "a_rb")
        free[("tb", bk)] = [t3]
        tok_rb[H] = t3

    def values(H):
        w = tok_pt[H] + [tok_v[H // 4]] + fr("o_bank")
        for k in range(8):
            t = mm3(bank(4), vsb[:, 0, k * 128:k * 128 + 128], vsb[:, 1, k * 128:k * 128 + 128],
                    pth[:, k, :], ptl[:, k, :], k == 0, k == 7, w, "t_av" if k == 7 else None)
        free["pt"] = [t]
        if H % 4 == 3:
            free["v"] = [t]
        return t

    tok_o = {}

    def o_out(H, t):
        t2 = tt(ta[:, :], bank(4), rb[:, :], ALU.mult, [t, tok_rb[H]] + fr("ta"), "v_o")
        free["o_bank"] = free["rb"] = [t2]
        j, i = (H // 2) % 2, H % 2
        w = fr(("o", j))
        th = copy_hi(osb[:, j, i, 0, :], ta[:, :], [t2] + w, "a_o")
        tl = sub_lo(DV, osb[:, j, i, 1, :], ta[:, :], osb[:, j, i, 0, :], [th] + w, "v_olo")
        free["ta"] = [tl]
        tok_o[H] = [th, tl]

    tok_x3 = {}

    def wo_part(q, i):
        j, nh = (q - 2) // 2, q % 2
        if q < 2 or j >= 32:
            return
        b = j // 16
        for hd in range(2):
            t = mm3(bank(6), osb[:, j % 2, hd, 0, i * 128:i * 128 + 128], osb[:, j % 2, hd, 1, i * 128:i * 128 + 128],
                    woh[:, nh, hd, :], wol[:, nh, hd, :], hd == 0, hd == 1,
                    tok_wo[q] + tok_o[2 * j] + tok_o[2 * j + 1] + (fr(("b", 6)) if hd == 0 else []),
                    "t_wo" if hd else None)
        if i == 3:
            free[("wo", nh)] = [t]
            if nh:
                free[("o", j % 2)] = [t]
        xs = xa[:, i, nh * 512:nh * 512 + 512]
        t = tt(xs, bank(6), xs, ALU.add, [t, tok_xa[(b, i)]], "v_xa")
        free[("b", 6)] = [t]
        if j % 16 == 15 and nh:
            tok_x3[b * 4 + i] = dma(x3_d[b * 4 + i], xa[:, i, :], [t], f"d_xs{i}")
            if b == 0:
                tok_xa[(1, i)] = dma(xa[:, i, :], x2_d[4 + i], [tok_x3[i], tok_x2[4 + i]], f"d_xa{i}")

    free[("k", 0)] = free[("k", 1)] = edge_w
    load_k(0)
    load_mask(0, 0, edge_w)
    load_h(0, 2, edge_h)
    load_h(0, 3, edge_h)
    t_cq = [dma(cosq[:, :], A["cosq"], edge_w, "d_cosq"), dma(sinq[:, :], A["sinq"], edge_w, "d_sinq")]
    q_part(0, 0, 7)
    q_part(0, 2, 7)
    load_mask(0, 1, edge_w)
    q_part(1, 0, 6)
    q_part(1, 2, 6)
    h3_out(7)
    edge = edge_w + edge_h + [("v_klo", Q.count["v_klo"]), ("v_h2", Q.count["v_h2"]), ("v_tl", Q.count["v_tl"]),
                              ("p_klo", Q.count["p_klo"]), ("t_htr", Q.count["t_htr"]),
                              ("d_khl0", Q.count["d_khl0"]), ("d_khl1", Q.count["d_khl1"])]
    for key in [("p", 0), ("p", 1), ("p", 2), ("q", 0), ("q", 1)]:
        free[key] = edge_w
    for key in ["v", "pt", ("o", 0), ("o", 1), ("wo", 0), ("wo", 1), "ua", "ta", "rb"]:
        free[key] = edge
    free[("tb", 2)], free[("tb", 3)] = fr(("b", 2)), fr(("b", 3))
    free["s_bank"] = fr(("b", 0)) + fr(("b", 1))
    free["o_bank"] = fr(("b", 4))
    load_wq(3)
    for i in range(2, 4):
        load_mask(0, i, edge_w)
    load_v(0)
    for i in range(4):
        tok_xa[(0, i)] = dma(xa[:, i, :], x2_d[i], [tok_x2[i]] + edge, f"d_xa{i}")
    q_part(0, 4, 7)
    q_end(0, q_part(0, 6, 7), 7)
    q_part(1, 4, 6)
    t = q_part(1, 6, 6)
    load_wq(4)
    load_wq(5)
    q_end(1, t, 6)
    free[("tb", 7)] = fr(("b", 7))
    scores(0, 0)
    scores(0, 1)

    n3 = [0]
    tok_up, t_x3, tok_ag = {}, {}, []
    pend3 = {}

    def up(k, hl):
        t, j = [(upa, 0), (upa, 1), (upb, 0), (upc, 0), (upc, 1), (upd, 0), (upe, 0), (upe, 1)][k]
        return t[:, j, hl, :]

    def load_up(k, w):
        r = n3[0] % 2
        n3[0] += 1
        d = dma(raw3[:, r, :], A["up"][k], fr(("ar", 2 * r)) + fr(("ar", 2 * r + 1)), f"d_r3{r}")
        h = copy_hi(up(k, 0), raw3[:, r, :], [d] + w, "a_up")
        l = sub_lo(PO, up(k, 1), raw3[:, r, :], up(k, 0), [h] + w, "p_up")
        free[("ar", 2 * r)] = free[("ar", 2 * r + 1)] = [l]
        tok_up[k] = [h, l]

    def load_x3(i, w=()):
        sl = i % 3
        t_x3[i] = dma(x3[:, sl, :], x3_d[i], [tok_x3[i]] + list(w) + fr(("x3", sl)), f"d_x3{sl}")

    tok_h4, tok_z, tok_zt, tok_n = {}, {}, {}, {}

    def norm3(i):
        tok_n[i] = layernorm(x3[:, i % 3, :], h4[:, i % 2, :], [t_x3[i]], fr(("h4", i % 2)), "v_h4")

    def trans3(i):
        sl = i % 2
        for j in range(8):
            t2 = transpose(ps[:, 2 + j // 4, (j % 4) * 128:(j % 4) * 128 + 128], h4[:, sl, j * 128:j * 128 + 128],
                           identf[:, :], [tok_n[i]] + fr(("tb", 2)) + fr(("tb", 3)), "t_h4" if j == 7 else None)
        free[("h4", sl)] = [t2]
        src = pair(2).rearrange("p (k t) -> p k t", k=8)
        w = fr(("h4t", sl))
        th = copy_hi(h4h[:, sl, :, :], src, [t2] + w, "a_h4")
        tl = sub_lo(DV, h4l[:, sl, :, :], src, h4h[:, sl, :, :], [th] + w, "v_h4l")
        free[("tb", 2)] = free[("tb", 3)] = [tl]
        tok_h4[i] = [th, tl]

    def gate(i):
        sl = i % 2
        for k in range(8):
            t = mm3(ps[:, 7, 0:36], h4h[:, sl, k, :], h4l[:, sl, k, :], agh[:, k, :], agl[:, k, :], k == 0, k == 7,
                    tok_h4[i] + tok_ag + fr(("tb", 7)), "t_g" if k == 7 else None)
        g = g_sb[:, sl, :]
        t = tt(g[:, 0:4], ps[:, 7, 32:36], eb[:, 0:4], ALU.add, [t, t_eb] + fr(("g", sl)), "v_g")
        t = op(DV, lambda e: e.reduce_max(g[:, 4:5], g[:, 0:4], AX), [t], "v_g")
        t = tsc(g[:, 8:12], g[:, 0:4], g[:, 4:5], None, ALU.is_equal, None, [t], "v_g")
        t = op(DV, lambda e: e.tensor_tensor_scan(g[:, 12:16], eb[:, 4:8], g[:, 8:12], 0.0, ALU.mult, ALU.add),
               [t], "v_g")
        t = stt(g[:, 16:20], g[:, 12:16], 1.0, g[:, 8:12], ALU.is_equal, ALU.mult, [t], "v_g")
        t = tt(zs[:, sl, 0:32].rearrange("p (e r) -> p e r", e=4), ps[:, 7, 0:32].rearrange("p (e r) -> p e r", e=4),
               g[:, 16:20].unsqueeze(2).broadcast_to([128, 4, 8]), ALU.mult, [t, t_zz] + fr(("zs", sl)), "v_z")
        free[("tb", 7)] = [t]
        free[("g", sl)] = [t]
        tok_z[i] = t

    def before_three(p):
        nonlocal t_eb, t_zz, t_lbz, t_lb
        if p == 62:
            w = [("t_q", Q.count["t_q"])]
            for k in range(4):
                load_up(k, w)
            d = dma(ag_raw[:, :], A["ag"], w, "d_ag")
            agf, agf2 = agh[:, :, :].rearrange("p a b -> p (a b)"), agl[:, :, :].rearrange("p a b -> p (a b)")
            th = copy_hi(agf, ag_raw[:, :], [d], "a_ag")
            tok_ag.extend([th, sub_lo(PO, agf2, ag_raw[:, :], agf, [th], "p_ag")])
        if p == 63:
            load_up(4, [("t_q", Q.count["t_q"])])
            load_up(5, fr(("k", 0)))
            w = [("v_max", Q.count["v_max"])]
            for i in range(3):
                load_x3(i, w)
            d0 = op(DV, lambda e: e.memset(lbr[:, :], 0.0), w, "v_lbz")
            t_lb = dma(lbr[0:32, :], A["lb"], [d0], "d_lb")
            for sl in range(2):
                free[("h4", sl)] = fr(("k", 1))
                free[("h4t", sl)] = [("t_p", Q.count["t_p"]), ("v_qr", Q.count["v_qr"])]
        if p == 64:
            w = fr("pt")
            load_up(6, w)
            load_up(7, w)
            th = copy_hi(lbh[:, :], lbr[:, :], [t_lb] + w, "a_lb")
            tok_lb.extend([th, sub_lo(PO, lbl[:, :], lbr[:, :], lbh[:, :], [th], "p_lb")])
            t_eb = dma(eb[:, :], A["eb"], w, "d_eb")
            t_zz = op(DV, lambda e: e.memset(zs[:, :, :], 0.0), w, "v_zz")
            for sl in range(2):
                free[("y", sl)] = free[("zt", sl)] = free[("g", sl)] = free[("zs", sl)] = w
            norm3(0)
            norm3(1)

    t_eb = t_zz = t_lbz = t_lb = None
    tok_lb = []

    for p in range(66):
        if p % 4 == 0:
            load_k(p // 4 + 1)
        if 1 <= p and p + 2 < 64:
            load_wq(2 * (p + 2) + 2) if p > 0 else None
        elif p == 0:
            load_wq(6)
        load_wo(p + 1)
        if 1 <= p <= 64:
            o_out(p - 1, values(p - 1))
            if (p - 1) % 4 == 3:
                load_v((p - 1) // 4 + 1)
        for w in range(4):
            if w == 3 and p < 64:
                inverse(p)
            if p < 64:
                p_turn(p, w, 0)
                if w == 3:
                    p_turn(p, w, 1)
            if p < 64:
                if p + 2 < 64:
                    tq = q_part(p + 2, 2 * w)
                if w < 3:
                    p_turn(p, w, 1)
                if w == 1 and p + 2 < 64:
                    load_wq(2 * (p + 2) + 3)
            if p == 65 and w in (0, 2):
                trans3(w // 2)
            if p == 65 and w in (1, 3):
                gate(w // 2)
            if w:
                wo_part(p, w)
            if w == 3 and p < 64:
                inverse_rows(p)
            if w < 2:
                if p < 64:
                    scores(p, w + 2)
                if w == 0:
                    wo_part(p, w)
            elif p + 1 < 64:
                scores(p + 1, w - 2)
        if p + 2 < 64:
            q_end(p + 2, tq)
        before_three(p)

    for bk in (0, 1, 4, 5):
        free[("b", bk)] = fr("s_bank") + fr("o_bank") + fr(("b", 5))

    def z_turn(i):
        sl = i % 2
        t = transpose(ps[:, 6, 0:128], zs[:, sl, :], identf[:, :], [tok_z[i]] + fr(("b", 6)), "t_z")
        free[("zs", sl)] = [t]
        w = fr(("zt", sl))
        th = copy_hi(zth[:, sl, :], ps[:, 6, 0:128], [t] + w, "a_z")
        tl = sub_lo(DV, ztl[:, sl, :], ps[:, 6, 0:128], zth[:, sl, :], [th] + w, "v_zl")
        free[("b", 6)] = [tl]
        tok_zt[i] = [th, tl]

    def main3(i, k, nh, bk):
        sl = i % 2
        mm3(bank(bk), h4h[:, sl, k, :], h4l[:, sl, k, :], up(k, 0)[:, nh * 512:nh * 512 + 512],
            up(k, 1)[:, nh * 512:nh * 512 + 512], k == 0, False,
            tok_up[k] + tok_h4[i] + (fr(("b", bk)) if k == 0 else []))

    tok_out = []

    def end3(i, bks):
        sl = i % 2
        for nh in range(2):
            t = mm3(bank(bks[nh]), zth[:, sl, :], ztl[:, sl, :], lbh[:, nh * 512:nh * 512 + 512],
                    lbl[:, nh * 512:nh * 512 + 512], False, True, tok_zt[i] + tok_lb, "t_l3")
            t2 = tt(y[:, sl, nh * 512:nh * 512 + 512], bank(bks[nh]), x3[:, i % 3, nh * 512:nh * 512 + 512], ALU.add,
                    [t, t_x3[i]] + fr(("y", sl)), "v_y")
            free[("b", bks[nh])] = [t2]
            tok_out.append(dma(out[i, :, nh * 512:nh * 512 + 512], y[:, sl, nh * 512:nh * 512 + 512], [t2],
                               f"d_y{sl}{nh}"))
        free[("h4t", sl)] = free[("zt", sl)] = [t]
        free[("x3", i % 3)] = [t2]
        free[("y", sl)] = tok_out[-2:]

    for i in range(8):
        bks = [[0, 1], [4, 5]][i % 2]
        if 1 <= i < 7:
            norm3(i + 1)
        for k in range(8):
            main3(i, k, 0, bks[0])
        if 1 <= i < 7:
            trans3(i + 1)
        z_turn(i)
        for k in range(8):
            main3(i, k, 1, bks[1])
        if 1 <= i < 7:
            gate(i + 1)
        end3(i, bks)
        if i + 3 < 8:
            load_x3(i + 3)
    Q.op(SP, lambda e: None, tok_out)

    block = ctx.enter_context(nc.Block())

    @block.sync
    def _(e):
        Q.emit(SP, e)

    @block.tensor
    def _(e):
        Q.emit(PE, e)

    @block.vector
    def _(e):
        Q.emit(DV, e)

    @block.scalar
    def _(e):
        Q.emit(AC, e)

    @block.gpsimd
    def _(e):
        Q.emit(PO, e)


def kernel(**inp):
    import ml_dtypes
    import numpy as np
    import concourse.bacc as bacc
    from concourse.bass_utils import run_bass_kernel_spmd as run

    def c(a):
        return np.ascontiguousarray(a)

    f = {k: np.asarray(v) for k, v in inp.items()}
    ctx = f["ctx_4096"]

    def slices(w, n):
        return c(w.reshape(8, 128, n, 128).transpose(2, 1, 0, 3).reshape(n, 128, 1024))

    def rows(w, m):
        return c(w.reshape(8, 128, m).transpose(1, 0, 2).reshape(128, 8 * m))

    inv = (np.float32(1.0) / (np.float64(10000.0) ** (np.arange(0, 128, 2, dtype=np.float32) / np.float32(128)))
           .astype(np.float32)).astype(np.float32)
    ang = (np.arange(1024, dtype=np.float32)[None, :] * inv[:, None]).astype(np.float32)
    cos, sin = np.cos(ang.astype(np.float64)), np.sin(ang.astype(np.float64))
    root = float(np.sqrt(np.float32(128.0)))
    cosk = np.concatenate([cos, cos], 0).astype(np.float32)
    sink = np.concatenate([sin, -sin], 0).astype(np.float32)
    cosq = (np.concatenate([cos, cos], 0)[:, :512] / root).astype(np.float32)
    sinq = (np.concatenate([sin, -sin], 0)[:, :512] / root).astype(np.float32)
    scal = np.concatenate([f[n].reshape(1) for n in
                           ("L0_xattn_x1_scale", "L0_xattn_x1_zp", "L0_xattn_x2_scale", "L0_xattn_x2_zp")])
    onehot = np.zeros((128, 8), np.float32)
    onehot[np.arange(128), np.arange(128) // 16] = 1
    rb = np.concatenate([np.tile(f["L0_ffn_router_b"][None, :], (128, 1)), onehot], 1)
    eb = np.concatenate([np.tile(f["L1_ffn_expert_bias"][None, :], (128, 1)), np.ones((128, 4), np.float32)], 1)
    arrays = {
        "identf": np.eye(128, dtype=np.float32),
        "identb": np.eye(128).astype(ml_dtypes.bfloat16),
        "onesb": np.ones((128, 128), ml_dtypes.bfloat16),
        "x": f["x"].reshape(8, 128, 1024),
        "ctx": ctx.reshape(2, 8, 128, 1024),
        "ctxT": ctx.transpose(0, 2, 1).reshape(2, 8, 128, 1024),
        "mask": f["mask_BxSxS2_ff0"].reshape(8, 128, 1024),
        "scal": np.tile(scal[None, :], (128, 1)),
        "cosk": cosk, "sink": sink, "cosq": cosq, "sinq": sinq,
        "wk": slices(f["L1_xattn_wk"], 8), "wv": slices(f["L1_xattn_wv"], 8), "wq": slices(f["L1_xattn_wq"], 32),
        "wo": f["L1_xattn_wo"].reshape(32, 128, 1024),
        "W": f["L0_ffn_W"].T.reshape(8, 128, 1024),
        "bias": np.tile(f["L0_ffn_b"][None, :], (128, 1)),
        "loraA": rows(f["L0_ffn_A"].reshape(128, 1024).T, 128),
        "loraB": f["L0_ffn_B"].transpose(0, 2, 1).reshape(128, 1024),
        "rw": rows(f["L0_ffn_router_W"].T, 8),
        "rb": rb, "eb": eb,
        "up": f["L1_ffn_W_up"].T.reshape(8, 128, 1024),
        "ag": rows(np.concatenate([f["L1_ffn_lora_A"].reshape(32, 1024).T, f["L1_ffn_gate_w"].T], 1), 36),
        "lb": f["L1_ffn_lora_B"].transpose(0, 2, 1).reshape(32, 1024),
    }
    nc = bacc.Bacc("TRN2", target_bir_lowering=False, num_devices=1)
    arrays = {"in_" + k: c(v) for k, v in arrays.items()}
    aps = {k[3:]: nc.dram_tensor(k, v.shape, mybir.dt.from_np(v.dtype), kind="ExternalInput").ap()
           for k, v in arrays.items()}
    o = nc.dram_tensor("out_0", (8, 128, 1024), F32, kind="ExternalOutput").ap()
    build(nc, aps, o)
    r = run(nc, [arrays], core_ids=[0])
    return r.results[0]["out_0"].reshape(2, 512, 1024)
```

```python
from contextlib import ExitStack

import concourse.bass as bass
from concourse import mybir

F32 = mybir.dt.float32
F32R = mybir.dt.float32r
BF16 = mybir.dt.bfloat16
ALU = mybir.AluOpType
ACT = mybir.ActivationFunctionType
AX = mybir.AxisListType.X

MAGIC = 12582912.0
EPS = 1e-5
LOWEST = -3.4028234663852886e38
SP, PE, DV, AC, PO = "sync", "tensor", "vector", "scalar", "gpsimd"


class Queues:

    def __init__(self, nc, ctx):
        self.nc, self.ctx = nc, ctx
        self.q = {e: [] for e in (SP, PE, DV, AC, PO)}
        self.sems, self.count = {}, {}

    def op(self, eng, fn, w=(), s=None, inc=1):
        for name, value in w:
            self.q[eng].append((name, value, None))
        if s is None:
            self.q[eng].append((None, 0, fn))
            return None
        if s not in self.sems:
            self.sems[s] = self.ctx.enter_context(self.nc.semaphore(s))
            self.count[s] = 0
        self.count[s] += inc
        sem = self.sems[s]
        self.q[eng].append((None, 0, lambda e: fn(e).then_inc(sem, inc)))
        return (s, self.count[s])

    def dma(self, dst, src, w=(), s=None, eng=SP):
        return self.op(eng, lambda e: e.dma_start(dst, src), w, s, 16)

    def emit(self, eng, e):
        seen = {}
        for name, value, fn in self.q[eng]:
            if fn is not None:
                fn(e)
            elif seen.get(name, 0) < value:
                seen[name] = value
                e.wait_ge(self.sems[name], value)


def fl(ap):
    return ap.rearrange("p a b -> p (a b)")


def f32(ap):
    return ap.bitcast(F32)


def build(nc, A, out):
    with ExitStack() as ctx:
        build_in(nc, ctx, A, out)


def build_in(nc, ctx, A, out):
    Q = Queues(nc, ctx)
    op, dma = Q.op, Q.dma

    def alloc(stack, name, shape, dt=F32):
        return stack.enter_context(nc.sbuf_tensor(name, shape, dt))

    ps = ctx.enter_context(nc.psum_tensor("ps", [128, 8, 512], F32))
    k_d = nc.dram_tensor("k_scratch", [16, 128, 2, 1024], F32, kind="Internal").ap()
    v_d = nc.dram_tensor("v_scratch", [16, 128, 2, 1024], F32, kind="Internal").ap()
    h_d = nc.dram_tensor("h_scratch", [2, 128, 8, 2, 512], F32, kind="Internal").ap()
    x2_d = nc.dram_tensor("x2_scratch", [8, 128, 1024], F32, kind="Internal").ap()
    x3_d = nc.dram_tensor("x3_scratch", [8, 128, 1024], F32, kind="Internal").ap()

    def bank(b):
        return ps[:, b, :]

    def pair(b):
        return fl(ps[:, b:b + 2, :])

    def copy_hi(dst, src, w, s):
        return op(AC, lambda e: e.copy(dst, src), w, s)

    def sub_lo(eng, dst, src, hi, w, s):
        return op(eng, lambda e: e.tensor_tensor(dst, src, f32(hi), ALU.subtract), w, s)

    def tt(dst, a, b, o, w, s, eng=DV):
        return op(eng, lambda e: e.tensor_tensor(dst, a, b, o), w, s)

    def tsc(dst, a, s1, s2, o1, o2, w, s):
        if o2 is None:
            return op(DV, lambda e: e.tensor_scalar(dst, a, s1, None, o1), w, s)
        return op(DV, lambda e: e.tensor_scalar(dst, a, s1, s2, o1, o2), w, s)

    def stt(dst, a, sc, b, o1, o2, w, s):
        return op(DV, lambda e: e.scalar_tensor_tensor(out=dst, in0=a, scalar=sc, in1=b, op0=o1, op1=o2), w, s)

    def mm(dst, l, r, start, stop, w=(), s=None):
        return op(PE, lambda e: e.matmul(dst, l, r, start=start, stop=stop), w, s)

    def mm3(dst, lh, ll, rh, rl, start, stop, w=(), s=None):
        mm(dst, ll, rh, start, False, w)
        mm(dst, lh, rl, False, False)
        return mm(dst, lh, rh, False, stop, (), s)

    def transpose(dst, src, ident, w=(), s=None):
        return op(PE, lambda e: e.transpose(dst, src, ident), w, s)

    identf = alloc(ctx, "identf", [128, 128])
    sm = alloc(ctx, "sm", [128, 4, 20])
    scal = alloc(ctx, "scal", [128, 16])
    small = alloc(ctx, "small", [128, 128])

    ln_n = [0]

    def layernorm(x, dst, w, wdst, s):
        c = sm[:, ln_n[0] % 4, :]
        ln_n[0] += 1
        op(DV, lambda e: e.bn_stats(c[:, 0:6], x[:, 0:512]), w)
        t = op(DV, lambda e: e.bn_stats(c[:, 6:12], x[:, 512:1024]), (), "v_ln")
        t = op(DV, lambda e: e.bn_aggr(c[:, 12:14], c[:, 0:12]), [t], "v_ln")
        t = tsc(c[:, 14:15], c[:, 13:14], EPS, None, ALU.add, None, [t], "v_ln")
        t = op(AC, lambda e: e.activation(c[:, 15:16], c[:, 14:15], ACT.Sqrt), [t], "a_sqrt")
        t = op(DV, lambda e: e.reciprocal(c[:, 16:17], c[:, 15:16]), [t], "v_ln")
        t = tsc(c[:, 17:18], c[:, 16:17], c[:, 16:17], c[:, 14:15], ALU.mult, ALU.mult, [t], "v_ln")
        t = tsc(c[:, 18:19], c[:, 17:18], -0.5, 1.5, ALU.mult, ALU.add, [t], "v_ln")
        t = tsc(c[:, 19:20], c[:, 18:19], c[:, 16:17], None, ALU.mult, None, [t], "v_ln")
        return tsc(dst, x, c[:, 12:13], c[:, 19:20], ALU.subtract, ALU.mult, [t] + wdst, s)

    def rope(src, cos, sin, u, t, w, wu, s):
        tt(u, src, cos, ALU.mult, w + wu, None)
        tt(t[0:64], src[64:128], sin[64:128], ALU.mult, (), None)
        return tt(t[64:128], src[0:64], sin[0:64], ALU.mult, (), s)

    NR = 3
    one = ExitStack()
    x_lo = alloc(one, "x_lo", [128, 4, 1024])
    raw = alloc(one, "raw", [128, NR, 1024])
    spare = alloc(one, "spare", [128, 2, 1024], F32R)
    x_hi = alloc(one, "x_hi", [128, 4, 1024])
    slots = alloc(one, "slots", [128, 8, 2, 1024], F32R)
    wh = alloc(one, "wh", [128, 2, 1024], F32R)
    wl = alloc(one, "wl", [128, 2, 1024], F32R)
    cosk = alloc(one, "cosk", [128, 1024])
    sink = alloc(one, "sink", [128, 1024])
    u_sb = alloc(one, "u_sb", [128, 2, 512])
    t_sb = alloc(one, "t_sb", [128, 512])
    khl = alloc(one, "khl", [128, 2, 2, 512], F32R)
    ctab = alloc(one, "ctab", [128, 1024])
    tmp = alloc(one, "tmp", [128, 3, 1024])
    ts_sb = alloc(one, "ts_sb", [128, 2, 512], F32R)
    l0 = ExitStack()
    identb = alloc(l0, "identb", [128, 128], BF16)
    onesb = alloc(l0, "onesb", [128, 128], BF16)
    bq = alloc(l0, "bq", [128, 8, 1024], BF16)
    a1T = alloc(l0, "a1T", [128, 8, 512], BF16)
    a_sb = alloc(l0, "a_sb", [128, 2, 1024], BF16)
    l0.close()
    h2 = ExitStack()
    h2h = alloc(h2, "h2h", [128, 8, 512], F32R)
    h2l = alloc(h2, "h2l", [128, 8, 512], F32R)
    h2.close()
    one.close()
    two = ExitStack()
    hTa = alloc(two, "hTa", [128, 4, 2, 512], F32R)
    wqh = alloc(two, "wqh", [128, 3, 512], F32R)
    wql = alloc(two, "wql", [128, 3, 512], F32R)
    araw = alloc(two, "araw", [128, 4, 512])
    hTb = alloc(two, "hTb", [128, 4, 2, 512], F32R)
    ksb = alloc(two, "ksb", [128, 2, 2, 1024], F32R)
    mask = alloc(two, "mask", [128, 4, 1024])
    cosq = alloc(two, "cosq", [128, 512])
    sinq = alloc(two, "sinq", [128, 512])
    psb = alloc(two, "psb", [128, 3, 1024])
    qsb = alloc(two, "qsb", [128, 2, 2, 512], F32R)
    pth = alloc(two, "pth", [128, 8, 512], F32R)
    ptl = alloc(two, "ptl", [128, 8, 512], F32R)
    vsb = alloc(two, "vsb", [128, 2, 1024], F32R)
    osb = alloc(two, "osb", [128, 2, 2, 2, 512], F32R)
    woh = alloc(two, "woh", [128, 2, 2, 512], F32R)
    wol = alloc(two, "wol", [128, 2, 2, 512], F32R)
    ua = alloc(two, "ua", [128, 512])
    ta = alloc(two, "ta", [128, 512])
    xa = alloc(two, "xa", [128, 4, 1024])
    st = alloc(two, "st", [128, 4, 16])
    two.close()
    three = ExitStack()
    upa = alloc(three, "upa", [128, 2, 2, 1024], F32R)
    upb = alloc(three, "upb", [128, 1, 2, 1024], F32R)
    ag_raw = alloc(three, "ag_raw", [128, 288])
    ag = alloc(three, "ag", [128, 8, 2, 36], F32R)
    alloc(three, "pad0", [128, 160])
    raw3 = alloc(three, "raw3", [128, 1024])
    alloc(three, "pad2", [128, 1024])
    upc = alloc(three, "upc", [128, 2, 2, 1024], F32R)
    upd = alloc(three, "upd", [128, 1, 2, 1024], F32R)
    h4 = alloc(three, "h4", [128, 2, 1024])
    x3 = alloc(three, "x3", [128, 3, 1024])
    lbr = alloc(three, "lbr", [128, 1024])
    h4h = alloc(three, "h4h", [128, 2, 8, 128], F32R)
    h4l = alloc(three, "h4l", [128, 2, 8, 128], F32R)
    alloc(three, "pad1", [128, 2048])
    upe = alloc(three, "upe", [128, 2, 2, 1024], F32R)
    lbh = alloc(three, "lbh", [128, 1024], F32R)
    lbl = alloc(three, "lbl", [128, 1024], F32R)
    y = alloc(three, "y", [128, 2, 1024])
    zs = alloc(three, "zs", [128, 2, 128])
    zth = alloc(three, "zth", [128, 2, 128], F32R)
    ztl = alloc(three, "ztl", [128, 2, 128], F32R)
    g_sb = alloc(three, "g_sb", [128, 2, 104])
    eb = alloc(three, "eb", [128, 8])
    three.close()

    def x_tile(i):
        return x_lo[:, i, :] if i < 4 else x_hi[:, i - 4, :]

    def slot(i, hl):
        s = i % 9
        if s == 6:
            return spare[:, hl, :]
        return slots[:, s if s < 6 else s - 1, hl, :]

    free = {}

    def fr(key):
        return list(free.get(key, []))

    raws = [(r, []) for r in range(NR)]

    def load_raw(src):
        r, wr = raws.pop(0)
        return r, dma(raw[:, r, :], src, wr, f"d_raw{r}")

    def load_split(src, hi, lo, w, eng=PO):
        return split_raw(load_raw(src), hi, lo, w, eng)

    def split_raw(loaded, hi, lo, w, eng):
        r, d = loaded
        h = copy_hi(hi, raw[:, r, :], [d] + w, "a_hi")
        l = sub_lo(eng, lo, raw[:, r, :], hi, [h] + w, "p_lo" if eng == PO else "v_lo")
        raws.append((r, [l]))
        return [h, l]

    tok_c = {}

    def load_c(i, eng=PO):
        src = A["ctxT"][i // 8, i % 8] if i < 16 else A["W"][i - 16]
        tok_c[i] = load_split(src, slot(i, 0), slot(i, 1), fr(("c", i % 9)), eng)

    units = [(b, g, kind) for b in range(2) for g in range(8) for kind in "kv"]
    tok_w = {}

    def load_w(n, eng=PO):
        if n < 32:
            b, g, kind = units[n]
            src = A["wk" if kind == "k" else "wv"][g]
        else:
            src = A["loraA"] if n == 32 else A["loraB"]
        tok_w[n] = load_split(src, wh[:, n % 2, :], wl[:, n % 2, :], fr(("w", n % 2)), eng)

    load_w(0)
    load_c(0, DV)
    load_w(1)
    for k in range(1, 8):
        load_c(k, DV if k % 2 else PO)
    t_cos = [dma(cosk[:, :], A["cosk"], (), "d_cosk"), dma(sink[:, :], A["sink"], (), "d_sink")]
    t_id = dma(identf[:, :], A["identf"], (), "d_identf")
    t_idb = [dma(identb[:, :], A["identb"], (), "d_identb"), dma(onesb[:, :], A["onesb"], (), "d_onesb")]
    w2_ahead = load_raw(A["wk"][1])
    t_sc = dma(scal[:, 0:4], A["scal"], (), "d_scal")
    t_x = {}
    for i in range(8):
        t_x[i] = [dma(x_tile(i), A["x"][i], (), f"d_x{i}")]

    tsc(scal[:, 6:7], scal[:, 1:2], -1.0, 128.0, ALU.mult, ALU.add, [t_sc], None)
    tsc(scal[:, 7:8], scal[:, 3:4], -1.0, 128.0, ALU.mult, ALU.add, (), None)
    op(DV, lambda e: e.reciprocal(scal[:, 4:5], scal[:, 0:1]))
    op(DV, lambda e: e.reciprocal(scal[:, 5:6], scal[:, 2:3]))
    t_s = tt(scal[:, 8:9], scal[:, 0:1], scal[:, 2:3], ALU.mult, (), "v_scal")
    t_s = tsc(scal[:, 9:10], scal[:, 6:7], scal[:, 7:8], 1024.0, ALU.mult, ALU.mult, [t_s], "v_scal")

    kv_n = [0]
    tok_kd, tok_vd = {}, {}
    late = []

    def kv_products(group):
        banks = [(kv_n[0] + j) % 4 for j in range(len(group))]
        last = {}
        for k in range(8):
            for j, (n, half) in enumerate(group):
                b, bk = units[n][0], banks[j]
                c = b * 8 + k
                rh = slot(c, 0)[:, half * 512:half * 512 + 512]
                rl = slot(c, 1)[:, half * 512:half * 512 + 512]
                lh, ll = wh[:, n % 2, k * 128:k * 128 + 128], wl[:, n % 2, k * 128:k * 128 + 128]
                end = n % 16 == 15 and half == 1
                last[j] = mm3(bank(bk), lh, ll, rh, rl, k == 0, k == 7,
                              tok_w[n] + tok_c[c] + (fr(("b", bk)) if k == 0 else []),
                              "t_kv" if k == 7 or end else None)
                if end:
                    free[("c", c % 9)] = [last[j]]
        for j, (n, half) in enumerate(group):
            free[("w", n % 2)] = [last[j]]
        return [(n, half, banks[j], last[j]) for j, (n, half) in enumerate(group)]

    stores = []

    def store(dst, o, w, toks):
        def issue():
            td = dma(dst, f32(khl[:, o, :, :]), w, f"d_khl{o}")
            free[("khl", o)] = [td]
            toks.append(td)
        stores.append(issue)

    def issue_stores():
        while stores:
            stores.pop(0)()

    def kv_store(n, half, bk, t):
        b, g, kind = units[n]
        o = kv_n[0] % 2
        kv_n[0] += 1
        u = u_sb[:, o, :]
        if kind == "k":
            cs = slice(half * 512, half * 512 + 512)
            tr = rope(bank(bk), cosk[:, cs], sink[:, cs], u, t_sb[:, :], [t] + t_cos + fr("t"), fr(("u", o)), "v_kr")
            free[("b", bk)] = [tr]
            tu = tt(u, u, t_sb[:, :], ALU.add, [tr], "p_ku", eng=PO)
            free["t"] = [tu]
            th = copy_hi(khl[:, o, 0, :], u, [tu] + fr(("khl", o)), "a_khi")
            tl = sub_lo(PO, khl[:, o, 1, :], u, khl[:, o, 0, :], [th] + fr(("khl", o)), "p_klo")
            free[("u", o)] = [tl]
            store(k_d[b * 8 + g, :, :, cs], o, [th, tl], tok_kd.setdefault(b * 8 + g, []))
            return
        tu = op(AC, lambda e: e.copy(u, bank(bk)), [t] + fr(("u", o)), "a_vt")
        free[("b", bk)] = [tu]

        vb = 6 - o if n < 24 else 6

        def finish():
            for j in range(4):
                t2 = transpose(ps[:, vb, j * 128:j * 128 + 128], u[:, j * 128:j * 128 + 128], identf[:, :],
                               [tu, t_id] + fr(("b", vb)), "t_vtr" if j == 3 else None)
            free[("u", o)] = [t2]
            th = copy_hi(khl[:, o, 0, :], bank(vb), [t2] + fr(("khl", o)), "a_khi")
            tl = sub_lo(DV, khl[:, o, 1, :], bank(vb), khl[:, o, 0, :], [th] + fr(("khl", o)), "v_klo")
            free[("b", vb)] = [tl]
            store(v_d[b * 8 + g, :, :, half * 512:half * 512 + 512], o, [th, tl], tok_vd.setdefault(b * 8 + g, []))

        late.append(finish)

    temps = [(tmp[:, k, :], []) for k in range(3)]

    def take():
        return temps.pop(0)

    def give(t, toks):
        temps.append((t, toks))

    R = small[:, 0:8]

    def quantise(q, src, rs, z, dst, w, wd, s):
        t = tsc(q, src, scal[:, rs:rs + 1], scal[:, z:z + 1], ALU.mult, ALU.add, w, "v_q")
        t2 = tsc(q, q, MAGIC, MAGIC, ALU.add, ALU.max, [t], "v_q")
        t3 = tsc(dst, q, MAGIC + 255.0, -(MAGIC + 128.0), ALU.min, ALU.add, [t2] + wd, s)
        return t, t3

    tok_a1T, tok_bq = [], {}
    n_a = [0]

    def background_x(b):
        pend = []
        for i in range(4):
            tile = b * 4 + i
            h, wh_ = take()
            th = layernorm(x_tile(tile), h, t_x[tile], wh_, "v_h")
            yield
            while pend:
                pend.pop(0)()
            a = n_a[0] % 2
            n_a[0] += 1
            av = a_sb[:, a, :]
            _, ta_ = quantise(h, h, 4, 1, av, [th, t_s], fr(("a", a)), "v_a")
            give(h, [ta_])
            t = op(AC, lambda e, av=av, tile=tile: e.activation(av, av, ACT.Copy, accum_out=R[:, tile:tile + 1]),
                   [ta_], "a_rs")
            tsc(R[:, tile:tile + 1], R[:, tile:tile + 1], scal[:, 7:8], None, ALU.mult, None, [t], "v_rs")

            def turn(i=i, a=a, t=t):
                pb = bank(7).bitcast(BF16)
                for k8 in range(8):
                    t2 = transpose(pb[:, k8 * 128:k8 * 128 + 128], a_sb[:, a, k8 * 128:k8 * 128 + 128], identb[:, :],
                                   [t] + t_idb + fr(("b", 7)), "t_atr" if k8 == 7 else None)
                free[("a", a)] = [t2]
                t2 = op(AC, lambda e: e.copy(a1T[:, :, i * 128:i * 128 + 128],
                                             pb.rearrange("p (k t) -> p k t", k=8)),
                        [t2] + fr("a1T"), "a_a1T")
                free[("b", 7)] = [t2]
                tok_a1T.append(t2)

            pend.append(turn)
            yield
        while pend:
            pend.pop(0)()

    def background_c(b):
        def load(k):
            return load_raw(A["ctx"][b, k])

        ahead = load(0)
        yield
        for k in range(8):
            r, d = ahead
            if k < 7:
                ahead = load(k + 1)
            _, tq = quantise(raw[:, r, :], raw[:, r, :], 5, 3, bq[:, k, :], [d, t_s], fr("bq"), "v_bq")
            raws.append((r, [tq]))
            tok_bq[k] = tq
            yield

    def l0_product(b):
        w = list(tok_a1T) + list(tok_bq.values()) + t_idb
        for nh in range(2):
            for k in range(8):
                t = mm(bank(4 + nh), onesb[:, :], bq[:, k, nh * 512:nh * 512 + 512], k == 0, k == 7,
                       w + fr(("b", 4 + nh)), "t_l0" if k == 7 else None)
            t_c = tsc(ctab[:, nh * 512:nh * 512 + 512], bank(4 + nh), scal[:, 6:7], scal[:, 9:10], ALU.mult, ALU.add,
                      [t], "v_ctab")
            free[("b", 4 + nh)] = [t_c]
        for n in range(8):
            i, nh = n // 2, n % 2
            tile, bk = b * 4 + i, 4 + n % 2
            for k in range(8):
                t = mm(bank(bk), a1T[:, k, i * 128:i * 128 + 128], bq[:, k, nh * 512:nh * 512 + 512],
                       k == 0, k == 7, fr(("b", bk)), "t_l0" if k == 7 else None)
            q, wq_ = take()
            xs = x_tile(tile)[:, nh * 512:nh * 512 + 512]
            t2 = stt(q[:, 0:512], bank(bk), R[:, tile:tile + 1], ctab[:, nh * 512:nh * 512 + 512], ALU.add, ALU.add,
                     [t, t_c] + wq_, "v_l0")
            free[("b", bk)] = [t2]
            t3 = stt(xs, q[:, 0:512], scal[:, 8:9], xs, ALU.mult, ALU.add, [t2], "v_l0")
            give(q, [t3])
            t_x[tile] = [t3]
        free["bq"] = free["a1T"] = [t]
        tok_a1T.clear()
        free["ctab"] = [t2]
        return t

    def finish_late():
        while late:
            late.pop(0)()

    def run_kv(ns, bx, bc=iter(())):
        ns = list(ns)
        if ns[0] % 16 == 0:
            groups = [[(ns[0], 0), (ns[0], 1), (ns[1], 0), (ns[1], 1)]]
            ns = ns[2:]
        else:
            groups = []
        groups += [[(n, half)] for n in ns for half in range(2)]
        for group in groups:
            if len(group) == 1 and group[0][1] == 0 and group[0][0] + 1 not in tok_w:
                load_w(group[0][0] + 1)
            issue_stores()
            done = kv_products(group)
            if group[0][0] == 0 and len(group) > 1:
                tok_w[2] = split_raw(w2_ahead, wh[:, 0, :], wl[:, 0, :], fr(("w", 0)), DV)
            elif len(group) > 1:
                load_w(group[-1][0] + 1, DV)
            several = len(late) > 1
            finish_late()
            if several:
                issue_stores()
            for u in done:
                if len(done) > 1:
                    issue_stores()
                kv_store(*u)
                if len(done) > 1:
                    continue
                next(bc if units[u[0]][2] == "k" else bx, None)
        for rest in (bc, bx):
            for _ in rest:
                pass

    run_kv(range(0, 16), background_x(0), background_c(0))
    finish_late()
    load_w(17)
    for k in range(8):
        load_c(8 + k)
    l0_product(0)
    run_kv(range(16, 26), background_x(1), background_c(1))
    finish_late()
    t_l0 = l0_product(1)
    w_h2 = [t_l0]
    t_bias = dma(ctab[:, :], A["bias"], fr("ctab"), "d_bias")
    t_rt = [dma(small[:, 64:128], A["rw"], (), "d_rw"), dma(small[:, 40:56], A["rb"], (), "d_rb")]
    tok_h2, tok_ts = {}, {}

    def ffn_norm(tile):
        h, w = take()
        t = layernorm(x_tile(tile), h, t_x[tile], w, "v_h")
        t_x[tile] = [tt(x_tile(tile), x_tile(tile), ctab[:, :], ALU.add, [t, t_bias], "p_xb", eng=PO)]
        return h, t

    def tile_transposes(h, t, bk=4):
        for j in range(8):
            t2 = transpose(ps[:, bk + j // 4, (j % 4) * 128:(j % 4) * 128 + 128], h[:, j * 128:j * 128 + 128],
                           identf[:, :], [t, t_id] + (fr(("b", bk)) + fr(("b", bk + 1)) if j == 0 else []),
                           "t_htr" if j == 7 else None)
        give(h, [t2])
        return t2

    def ffn_transposes(tile, h, t):
        i = tile % 4
        bk = 4 if tile < 4 else 6
        t2 = tile_transposes(h, t, bk)
        dst = h2h[:, :, i * 128:i * 128 + 128]
        src = pair(bk).rearrange("p (k t) -> p k t", k=8)
        w = w_h2 + fr(("h2", i))
        th = copy_hi(dst, src, [t2] + w, "a_h2")
        tl = sub_lo(DV, h2l[:, :, i * 128:i * 128 + 128], src, dst, [th] + w, "v_h2")
        free[("b", bk)] = free[("b", bk + 1)] = [tl]
        tok_h2[i] = [th, tl]

    def router(b):
        w = [x for v in tok_h2.values() for x in v]
        op(DV, lambda e: e.tensor_reduce(small[:, 8:16], f32(h2h[:, :, 179:511]), AX, ALU.add), w)
        t = op(DV, lambda e: e.tensor_reduce(small[:, 16:24], f32(h2l[:, :, 179:511]), AX, ALU.add), (), "v_rt")
        t = tt(small[:, 8:16], small[:, 8:16], small[:, 16:24], ALU.add, [t], "v_rt")
        qbc, wq_ = take()
        t_q = op(DV, lambda e: e.tensor_copy(qbc.rearrange("p (k m) -> p k m", k=8),
                                             small[:, 8:16].unsqueeze(2).broadcast_to([128, 8, 128])),
                 [t] + wq_, "v_rt")

        def end():
            for k in range(8):
                t2 = mm(ps[:, 6, 0:8], qbc[:, k * 128:k * 128 + 128], small[:, 64 + k * 8:72 + k * 8], k == 0, k == 7,
                        [t_q] + t_rt + fr(("b", 6)), "t_rt" if k == 7 else None)
            give(qbc, [t2])
            t = stt(small[:, 16:24], ps[:, 6, 0:8], 1.0 / 332.0, small[:, 40:48], ALU.mult, ALU.add, [t2], "v_rt")
            free[("b", 6)] = [t]
            t = op(DV, lambda e: e.reduce_max(small[:, 32:33], small[:, 16:24], AX), [t], "v_rt")
            t = tsc(small[:, 33:34], small[:, 32:33], -1.0, None, ALU.mult, None, [t], "v_rt")
            t = op(AC, lambda e: e.activation(small[:, 24:32], small[:, 16:24], ACT.Exp, bias=small[:, 33:34],
                                              accum_out=small[:, 34:35]), [t], "a_rt")
            t = op(DV, lambda e: e.reciprocal(small[:, 35:36], small[:, 34:35]), [t], "v_rt")
            t = op(DV, lambda e: e.tensor_tensor_reduce(out=small[:, 56:64], in0=small[:, 24:32],
                                                        in1=small[:, 48:56], scale=2.0, scalar=0.0, op0=ALU.mult,
                                                        op1=ALU.add, accum_out=small[:, 36:37]), [t], "v_rt")
            return tsc(small[:, 37 + b:38 + b], small[:, 36:37], small[:, 35:36], None, ALU.mult, None, [t], "v_rt")

        return end

    held, tok_r = {}, {}

    def background_ffn():
        for i in range(6):
            if i < 4:
                held[i] = ffn_norm(i)
            if i > 1:
                ffn_transposes(i - 2, *held[i - 2])
            yield
        end = router(0)
        yield
        yield
        tok_r[0] = end()
        held[4] = ffn_norm(4)
        yield
        held[5] = ffn_norm(5)
        yield

    steps = background_ffn()
    run_kv(range(26, 31), steps, steps)
    load_w(32)
    load_c(16)
    for half in range(2):
        issue_stores()
        done = kv_products([(31, half)])
        finish_late()
        kv_store(*done[0])
    t_kv_end = done[0][3]
    temps.append((cosk[:, :], [("v_kr", Q.count["v_kr"])]))
    for i in range(17, 19):
        load_c(i)
    load_w(33)

    def lora_t(b):
        for k in range(8):
            t = mm3(bank(7), wh[:, 0, k * 128:k * 128 + 128], wl[:, 0, k * 128:k * 128 + 128], h2h[:, k, :],
                    h2l[:, k, :], k == 0, k == 7,
                    tok_w[32] + [x for v in tok_h2.values() for x in v] + (fr(("b", 7)) if k == 0 else []),
                    "t_lt" if k == 7 else None)
        return t

    def lora_scale(b, t):
        u = u_sb[:, 0, :]
        t2 = tsc(u, bank(7), small[:, 37 + b:38 + b], None, ALU.mult, None, [t, tok_r[b]] + fr(("u", 0)), "v_ts")
        free[("b", 7)] = [t2]
        w = fr("ts")
        th = copy_hi(ts_sb[:, 0, :], u, [t2] + w, "a_ts")
        tl = sub_lo(DV, ts_sb[:, 1, :], u, ts_sb[:, 0, :], [th] + w, "v_tl")
        free[("u", 0)] = [tl]
        tok_ts[b] = [th, tl]

    tok_x2, tok_hd = {}, {}

    def ffn_main(i, k, nh, bk):
        return mm3(bank(bk), h2h[:, k, i * 128:i * 128 + 128], h2l[:, k, i * 128:i * 128 + 128],
                   slot(16 + k, 0)[:, nh * 512:nh * 512 + 512], slot(16 + k, 1)[:, nh * 512:nh * 512 + 512],
                   k == 0, False, tok_c[16 + k] + tok_h2[i] + (fr(("b", bk)) if k == 0 else []),
                   "t_fm" if k == 7 else None)

    def ffn_half(i, nh, bk):
        for k in range(8):
            t = ffn_main(i, k, nh, bk)
        if nh:
            free[("h2", i)] = [t]

    def ffn_end(b, i, bks):
        tile = b * 4 + i
        x = x_tile(tile)
        for nh in range(2):
            t = mm3(bank(bks[nh]), ts_sb[:, 0, i * 128:i * 128 + 128], ts_sb[:, 1, i * 128:i * 128 + 128],
                    wh[:, 1, nh * 512:nh * 512 + 512], wl[:, 1, nh * 512:nh * 512 + 512], False, True,
                    tok_w[33] + tok_ts[b], "t_fl")
            xs = x[:, nh * 512:nh * 512 + 512]
            t2 = tt(xs, bank(bks[nh]), xs, ALU.add, [t] + t_x[tile], "v_x2")
            free[("b", bks[nh])] = [t2]
        free["ts"] = [t]
        tok_x2[tile] = dma(x2_d[tile], x, [t2], f"d_x{tile}")
        h, w = take()
        t = layernorm(x, h, [t2], w, "v_h")
        held[("h3", tile)] = (h, t)
        return t

    def h3_out(tile):
        b, i = tile // 4, tile % 4
        t2 = tile_transposes(*held[("h3", tile)])
        for j in range(2):
            th = copy_hi(khl[:, j, 0, :], bank(4 + j), [t2] + fr(("khl", j)), "a_khi")
            tl = sub_lo(DV, khl[:, j, 1, :], bank(4 + j), khl[:, j, 0, :], [th], "v_klo")
            free[("b", 4 + j)] = [tl]
            for hl in range(2):
                td = dma(h_d[b, :, 4 * j:4 * j + 4, hl, i * 128:i * 128 + 128],
                         f32(khl[:, j, hl, :]).rearrange("p (k t) -> p k t", k=4), [tl, th], f"d_khl{j}")
            free[("khl", j)] = [td]
            tok_hd.setdefault(b, []).append(td)

    t = lora_t(0)
    issue_stores()
    finish_late()
    issue_stores()
    lora_scale(0, t)
    for i in range(19, 24):
        load_c(i)
    for k in range(8):
        for i in range(2):
            for nh in range(2):
                t = ffn_main(i, k, nh, 2 * i + nh)
    free[("h2", 0)] = free[("h2", 1)] = [t]
    ffn_end(0, 0, [0, 1])
    ffn_end(0, 1, [2, 3])
    ffn_half(2, 0, 0)
    ffn_transposes(4, *held[4])
    ffn_half(2, 1, 1)
    h3_out(0)
    ffn_end(0, 2, [0, 1])
    held[6] = ffn_norm(6)
    ffn_half(3, 0, 2)
    h3_out(1)
    ffn_transposes(5, *held[5])
    ffn_half(3, 1, 3)
    h3_out(2)
    ffn_transposes(6, *held[6])
    t_n3 = ffn_end(0, 3, [2, 3])
    held[7] = ffn_norm(7)
    ffn_half(0, 0, 0)
    h3_out(3)
    ffn_transposes(7, *held[7])
    ffn_half(0, 1, 1)
    end_r = router(1)
    t_lt = lora_t(1)
    tok_r[1] = end_r()
    lora_scale(1, t_lt)
    ffn_half(1, 0, 2)

    edge_x = [tok_x2[i] for i in range(4)] + [t_n3]
    edge_raw = [t for _, w in raws for t in w]
    tok_wq, tok_wo, tok_q, tok_h3 = {}, {}, {}, {}
    n_ar = [0]
    for r in range(4):
        free[("ar", r)] = [t_kv_end]
    for r in range(3):
        free[("wq", r)] = edge_raw

    splits = []
    shared = [True]

    def load_ahead(src, hi, lo, key, toks):
        r = n_ar[0] % 4 if shared[0] else 2 + n_ar[0] % 2
        n_ar[0] += 1
        d = dma(araw[:, r, :], src, fr(("ar", r)), f"d_ar{r}")

        def split():
            h = copy_hi(hi, araw[:, r, :], [d] + fr(key), "a_whi")
            l = sub_lo(PO, lo, araw[:, r, :], hi, [h] + fr(key), "p_wlo")
            free[("ar", r)] = [l]
            toks.extend([h, l])

        splits.append(split)

    def issue_split():
        if splits:
            splits.pop(0)()

    def load_wq(n, ahead=False):
        if n >= 128:
            return
        head, half = (n // 2) % 32, n % 2
        sl = n % 3
        tok_wq[n] = []
        load_ahead(A["wq"][head, :, half * 512:half * 512 + 512], wqh[:, sl, :], wql[:, sl, :], ("wq", sl), tok_wq[n])
        if not ahead:
            issue_split()

    def hT(k, hl):
        return hTa[:, k, hl, :] if k < 4 else hTb[:, k - 4, hl, :]

    def load_h(b, w, wt):
        dst = hTa[:, 2 * w:2 * w + 2, :, :] if w < 2 else hTb[:, 2 * w - 4:2 * w - 2, :, :]
        tok_h3[(b, w)] = dma(f32(dst), h_d[b, :, 2 * w:2 * w + 2, :, :], tok_hd[b] + wt, f"d_h{w}")

    ffn_end(1, 0, [0, 1])
    load_h(0, 0, edge_x)
    load_wq(0)
    ffn_half(1, 1, 3)
    h3_out(4)
    t_n5 = ffn_end(1, 1, [2, 3])
    load_h(0, 1, edge_x)
    load_wq(1)
    ffn_half(2, 0, 0)
    ffn_half(2, 1, 1)
    h3_out(5)
    ffn_end(1, 2, [0, 1])
    load_wq(2)
    load_h(0, 2, [t_n5, tok_x2[4], tok_x2[5]])
    for n in range(3, 6):
        load_wq(n, True)
    ffn_half(3, 0, 2)
    ffn_half(3, 1, 3)
    h3_out(6)
    ffn_end(1, 3, [2, 3])

    edge_w = [("t_fl", Q.count["t_fl"])]
    edge_h = [("v_h", Q.count["v_h"]), ("p_xb", Q.count["p_xb"])] + [tok_x2[i] for i in range(4, 8)]

    def load_wo(q):
        j, nh = (q - 2) // 2, q % 2
        if q < 2 or j >= 32:
            return
        tok_wo[q] = []
        for i in range(2):
            head = (2 * j + i) % 32
            load_ahead(A["wo"][head, :, nh * 512:nh * 512 + 512], woh[:, nh, i, :], wol[:, nh, i, :], ("wo", nh),
                       tok_wo[q])

    tok_k, tok_v, tok_m, tok_xa = {}, {}, {}, {}

    def load_k(G):
        if G < 16:
            tok_k[G] = dma(f32(ksb[:, G % 2, :, :]), k_d[G], tok_kd[G] + fr(("k", G % 2)), f"d_k{G % 2}")

    def load_v(G):
        if G < 16:
            tok_v[G] = dma(f32(vsb[:, :, :]), v_d[G], tok_vd[G] + fr("v"), "d_v")

    def load_mask(b, i, w):
        tok_m[(b, i)] = dma(mask[:, i, :], A["mask"][b * 4 + i], w, f"d_m{i}")

    def q_part(H, k, bk=5):
        for k in (k, k + 1):
            n = 2 * H + k // 4
            sl = n % 3
            c = (k % 4) * 128
            t = mm3(bank(bk), wqh[:, sl, c:c + 128], wql[:, sl, c:c + 128], hT(k, 0), hT(k, 1),
                    k == 0, k == 7, tok_wq[n] + [tok_h3[(H // 32, k // 2)]] + (fr(("b", bk)) if k == 0 else []),
                    "t_q" if k % 2 else None)
        if k % 4 == 3:
            free[("wq", (2 * H + k // 4) % 3)] = [t]
        if H == 31:
            load_h(1, k // 2, [t])
        return t

    def q_end(H, t, bk=5):
        o = H % 2
        tr = rope(bank(bk), cosq[:, :], sinq[:, :], ua[:, :], ta[:, :], [t] + t_cq + fr("ta"), fr("ua"), "v_qr")
        free[("b", bk)] = [tr]
        tu = tt(ua[:, :], ua[:, :], ta[:, :], ALU.add, [tr], "p_qu", eng=PO)
        free["ta"] = [tu]
        w = fr(("q", o))
        th = copy_hi(qsb[:, o, 0, :], ua[:, :], [tu] + w, "a_qhi")
        tl = sub_lo(PO, qsb[:, o, 1, :], ua[:, :], qsb[:, o, 0, :], [th] + w, "p_qlo")
        free["ua"] = [tl]
        tok_q[H] = [th, tl]

    n_p = [0]
    tok_p, tok_pt = {}, {}

    def scores(H, i):
        b, G, o = H // 32, H // 4, H % 2
        for nh in range(2):
            t = mm3(bank(nh), qsb[:, o, 0, i * 128:i * 128 + 128], qsb[:, o, 1, i * 128:i * 128 + 128],
                    ksb[:, G % 2, 0, nh * 512:nh * 512 + 512], ksb[:, G % 2, 1, nh * 512:nh * 512 + 512], True, True,
                    tok_q[H] + [tok_k[G]] + fr("s_bank"), "t_s" if nh else None)
        if i == 3:
            free[("q", o)] = [t]
            if H % 4 == 3:
                free[("k", G % 2)] = [t]
        r = n_p[0] % 3
        n_p[0] += 1
        P = psb[:, r, :]
        c = st[:, H % 4, :]
        tm = op(DV, lambda e: e.tensor_tensor_reduce(out=P, in0=pair(0), in1=mask[:, i, :], scale=1.0,
                                                     scalar=LOWEST, op0=ALU.add, op1=ALU.max,
                                                     accum_out=c[:, i:i + 1]),
                [t, tok_m[(b, i)]] + fr(("p", r)), "v_max")
        free["s_bank"] = [tm]
        if H == 31:
            load_mask(1, i, [tm])
        tn = tsc(c[:, 4 + i:5 + i], c[:, i:i + 1], -1.0, None, ALU.mult, None, [tm], "v_nmax")

        def exp():
            te = op(AC, lambda e: e.activation(P, P, ACT.Exp, bias=c[:, 4 + i:5 + i], accum_out=c[:, 8 + i:9 + i]),
                    [tn, tm], "a_exp")
            tok_p[(H, i)] = (r, te)

        exps.append(exp)

    exps = []

    def issue_exp():
        while exps:
            exps.pop(0)()

    def normalise(H, i):
        r, te = tok_p[(H, i)]
        P = psb[:, r, :]
        c = st[:, H % 4, :]
        t = op(DV, lambda e: e.reciprocal(c[:, 12 + i:13 + i], c[:, 8 + i:9 + i]), [te], "v_rinv")
        tok_p[(H, i)] = (r, tsc(P, P, c[:, 12 + i:13 + i], None, ALU.mult, None, [t], "v_p"))

    turn_banks = [2, 3, 7]
    n_tb = [0]

    def next_turn_bank():
        bk = turn_banks[n_tb[0] % 3]
        n_tb[0] += 1
        return bk

    def p_turn(H, i, half):
        r, te = tok_p[(H, i)]
        bk = next_turn_bank()
        for k in range(4):
            c = (half * 4 + k) * 128
            t = transpose(ps[:, bk, k * 128:k * 128 + 128], psb[:, r, c:c + 128],
                          identf[:, :], [te] + fr(("tb", bk)), "t_p" if k == 3 else None)
        free[("p", r)] = [t]
        src = bank(bk).rearrange("p (k t) -> p k t", k=4)
        ks, qs = slice(half * 4, half * 4 + 4), slice(i * 128, i * 128 + 128)
        w = fr("pt")
        th = copy_hi(pth[:, ks, qs], src, [t] + w, "a_pt")
        tl = sub_lo(DV, ptl[:, ks, qs], src, pth[:, ks, qs], [th] + w, "v_pt")
        free[("tb", bk)] = [tl]
        tok_pt.setdefault(H, []).extend([th, tl])

    def values(H):
        w = tok_pt[H] + [tok_v[H // 4]] + fr("o_bank")
        for k in range(8):
            t = mm3(bank(4), vsb[:, 0, k * 128:k * 128 + 128], vsb[:, 1, k * 128:k * 128 + 128],
                    pth[:, k, :], ptl[:, k, :], k == 0, k == 7, w, "t_av" if k == 7 else None)
        free["pt"] = [t]
        if H % 4 == 3:
            free["v"] = [t]
        return t

    tok_o = {}

    def o_out(H, t):
        j, i = (H // 2) % 2, H % 2
        w = fr(("o", j))
        th = copy_hi(osb[:, j, i, 0, :], bank(4), [t] + w, "a_o")
        tl = sub_lo(DV, osb[:, j, i, 1, :], bank(4), osb[:, j, i, 0, :], [th] + w, "v_olo")
        free["o_bank"] = [tl]
        tok_o[H] = [th, tl]

    tok_x3 = {}

    def wo_part(q, i):
        j, nh = (q - 2) // 2, q % 2
        if q < 2 or j >= 32:
            return
        b = j // 16
        bk, key = (4, "o_bank") if i in (1, 2) else (6, ("b", 6))
        for hd in range(2):
            t = mm3(bank(bk), osb[:, j % 2, hd, 0, i * 128:i * 128 + 128], osb[:, j % 2, hd, 1, i * 128:i * 128 + 128],
                    woh[:, nh, hd, :], wol[:, nh, hd, :], hd == 0, hd == 1,
                    tok_wo[q] + tok_o[2 * j] + tok_o[2 * j + 1] + (fr(key) if hd == 0 else []),
                    "t_wo" if hd else None)
        if i == 3:
            free[("wo", nh)] = [t]
            if nh:
                free[("o", j % 2)] = [t]
        xs = xa[:, i, nh * 512:nh * 512 + 512]
        t = tt(xs, bank(bk), xs, ALU.add, [t, tok_xa[(b, i)]], "v_xa")
        free[key] = [t]
        if j % 16 == 15 and nh:
            tok_x3[b * 4 + i] = dma(x3_d[b * 4 + i], xa[:, i, :], [t], f"d_xs{i}")
            if b == 0:
                tok_xa[(1, i)] = dma(xa[:, i, :], x2_d[4 + i], [tok_x3[i], tok_x2[4 + i]], f"d_xa{i}")

    free[("k", 0)] = free[("k", 1)] = edge_w
    load_h(0, 3, edge_h)
    t_cq = [dma(cosq[:, :], A["cosq"], edge_w, "d_cosq"), dma(sinq[:, :], A["sinq"], edge_w, "d_sinq")]
    load_k(0)
    load_mask(0, 0, edge_w)
    q_part(0, 0, 7)
    q_part(0, 2, 7)
    issue_split()
    q_part(1, 0, 6)
    q_part(1, 2, 6)
    h3_out(7)
    edge = edge_w + edge_h + [("v_klo", Q.count["v_klo"]), ("v_h2", Q.count["v_h2"]), ("v_tl", Q.count["v_tl"]),
                              ("p_klo", Q.count["p_klo"]), ("t_htr", Q.count["t_htr"]),
                              ("d_khl0", Q.count["d_khl0"]), ("d_khl1", Q.count["d_khl1"])]
    for key in [("p", 0), ("p", 1), ("p", 2), ("q", 0), ("q", 1), "ua", "ta"]:
        free[key] = edge_w
    for key in ["v", "pt", ("o", 0), ("o", 1), ("wo", 0), ("wo", 1)]:
        free[key] = edge
    free[("tb", 2)], free[("tb", 3)] = fr(("b", 2)), fr(("b", 3))
    free["s_bank"] = fr(("b", 0)) + fr(("b", 1))
    free["o_bank"] = fr(("b", 4))
    for i in range(1, 4):
        load_mask(0, i, edge_w)
    q_part(0, 4, 7)
    q_part(1, 4, 6)
    q_end(0, q_part(0, 6, 7), 7)
    issue_split()
    t = q_part(1, 6, 6)
    q_end(1, t, 6)
    issue_split()
    free[("tb", 7)] = fr(("b", 7))
    scores(0, 0)
    issue_exp()
    scores(0, 1)
    normalise(0, 0)

    tok_up, t_x3, tok_ag = {}, {}, []
    pend3 = {}

    def up(k, hl):
        t, j = [(upa, 0), (upa, 1), (upb, 0), (upc, 0), (upc, 1), (upd, 0), (upe, 0), (upe, 1)][k]
        return t[:, j, hl, :]

    def load_up(k):
        tok_up[k] = dma(raw3[:, :], A["up"][k], fr(("ar", 0)) + fr(("ar", 1)), "d_r3")

    def split_up(k, w):
        d = tok_up[k]
        h = copy_hi(up(k, 0), raw3[:, :], [d] + w, "a_up")
        l = sub_lo(PO, up(k, 1), raw3[:, :], up(k, 0), [h] + w, "p_up")
        free[("ar", 0)] = free[("ar", 1)] = [l]
        tok_up[k] = [h, l]

    def load_x3(i, w=()):
        sl = i % 3
        t_x3[i] = dma(x3[:, sl, :], x3_d[i], [tok_x3[i]] + list(w) + fr(("x3", sl)), f"d_x3{sl}")

    tok_h4, tok_z, tok_zt, tok_n = {}, {}, {}, {}

    def norm3(i):
        tok_n[i] = layernorm(x3[:, i % 3, :], h4[:, i % 2, :], [t_x3[i]], fr(("h4", i % 2)), "v_h4")

    def trans3(i):
        sl = i % 2
        for j in range(8):
            t2 = transpose(ps[:, 2 + j // 4, (j % 4) * 128:(j % 4) * 128 + 128], h4[:, sl, j * 128:j * 128 + 128],
                           identf[:, :], [tok_n[i]] + fr(("tb", 2)) + fr(("tb", 3)), "t_h4" if j == 7 else None)
        free[("h4", sl)] = [t2]
        src = pair(2).rearrange("p (k t) -> p k t", k=8)
        w = fr(("h4t", sl))
        th = copy_hi(h4h[:, sl, :, :], src, [t2] + w, "a_h4")
        tl = sub_lo(DV, h4l[:, sl, :, :], src, h4h[:, sl, :, :], [th] + w, "v_h4l")
        free[("tb", 2)] = free[("tb", 3)] = [tl]
        tok_h4[i] = [th, tl]

    def gate(i):
        sl = i % 2
        w = tok_h4[i] + tok_ag + fr(("tb", 7))
        for k in range(8):
            mm(ps[:, 7, 0:72], h4h[:, sl, k, :], ag[:, k, :, :].rearrange("p a b -> p (a b)"), k == 0, False, w)
            t = mm(ps[:, 7, 0:36], h4l[:, sl, k, :], ag[:, k, 0, :], False, k == 7, (), "t_g" if k == 7 else None)
        g = g_sb[:, sl, :]
        t = op(AC, lambda e: e.copy(g[:, 68:104], ps[:, 7, 36:72]), [t] + fr(("g", sl)), "a_g")
        t = tt(g[:, 32:68], ps[:, 7, 0:36], g[:, 68:104], ALU.add, [t], "v_g")
        free[("tb", 7)] = [t]
        t = tt(g[:, 0:4], g[:, 64:68], eb[:, 0:4], ALU.add, [t, t_eb], "v_g")
        t = op(DV, lambda e: e.reduce_max(g[:, 4:5], g[:, 0:4], AX), [t], "v_g")
        t = tsc(g[:, 8:12], g[:, 0:4], g[:, 4:5], None, ALU.is_equal, None, [t], "v_g")
        t = op(DV, lambda e: e.tensor_tensor_scan(g[:, 12:16], eb[:, 4:8], g[:, 8:12], 0.0, ALU.mult, ALU.add),
               [t], "v_g")
        t = stt(g[:, 16:20], g[:, 12:16], 1.0, g[:, 8:12], ALU.is_equal, ALU.mult, [t], "v_g")
        t = tt(zs[:, sl, 0:32].rearrange("p (e r) -> p e r", e=4), g[:, 32:64].rearrange("p (e r) -> p e r", e=4),
               g[:, 16:20].unsqueeze(2).broadcast_to([128, 4, 8]), ALU.mult, [t, t_zz] + fr(("zs", sl)), "v_z")
        free[("g", sl)] = [t]
        tok_z[i] = t

    def main3(i, k, nh, bk):
        sl = i % 2
        mm3(bank(bk), h4h[:, sl, k, :], h4l[:, sl, k, :], up(k, 0)[:, nh * 512:nh * 512 + 512],
            up(k, 1)[:, nh * 512:nh * 512 + 512], k == 0, False,
            tok_up[k] + tok_h4[i] + (fr(("b", bk)) if k == 0 else []))

    def before_three(p):
        nonlocal t_eb, t_zz, t_lbz, t_lb
        if p == 62:
            w = [("t_q", Q.count["t_q"])]
            d = dma(ag_raw[:, :], A["ag"], w, "d_ag")
            tok_ag.append(d)
        if p == 63:
            w = [("v_max", Q.count["v_max"])]
            d0 = op(DV, lambda e: e.memset(lbr[:, :], 0.0), w, "v_lbz")
            t_lb = dma(lbr[0:32, :], A["lb"], [d0], "d_lb")
            for sl in range(2):
                free[("h4", sl)] = fr(("k", 1))
                free[("h4t", sl)] = [("t_p", Q.count["t_p"]), ("v_qr", Q.count["v_qr"])]
            norm3(0)
        if p == 64:
            w = fr("pt")
            th = copy_hi(lbh[:, :], lbr[:, :], [t_lb] + w, "a_lb")
            tok_lb.extend([th, sub_lo(PO, lbl[:, :], lbr[:, :], lbh[:, :], [th], "p_lb")])
            t_eb = dma(eb[:, :], A["eb"], w, "d_eb")
            t_zz = op(DV, lambda e: e.memset(zs[:, :, :], 0.0), w, "v_zz")
            for sl in range(2):
                free[("y", sl)] = free[("zt", sl)] = free[("g", sl)] = free[("zs", sl)] = w
            free[("b", 0)] = free[("b", 1)] = fr("s_bank")

    t_eb = t_zz = t_lbz = t_lb = None
    tok_lb = []

    up_at = {(62, 0): 0, (62, 1): 1, (62, 2): 2, (62, 3): 3, (63, 0): 4, (63, 2): 5, (64, 1): 6, (64, 3): 7}
    for p in range(66):
        if p == 62:
            shared[0] = False
            load_up(0)
        if p % 4 == 0:
            load_k(p // 4 + 1)
        if p + 2 < 64:
            load_wq(2 * (p + 2) + 2, True)
        load_wo(p + 1)
        if p + 2 < 64:
            load_wq(2 * (p + 2) + 3, True)
        if p == 0:
            load_v(0)
        if p == 1:
            for i in range(4):
                tok_xa[(0, i)] = dma(xa[:, i, :], x2_d[i], [tok_x2[i]] + edge_w, f"d_xa{i}")
        if 1 <= p <= 64:
            o_out(p - 1, values(p - 1))
            if (p - 1) % 4 == 3:
                load_v((p - 1) // 4 + 1)
        for w in range(4):
            if p < 64:
                p_turn(p, w, 0)
                if w == 3:
                    p_turn(p, w, 1)
                issue_exp()
                if w < 3:
                    normalise(p, w + 1)
            if p < 64:
                if p + 2 < 64:
                    tq = q_part(p + 2, 2 * w)
                if w < 3:
                    p_turn(p, w, 1)
            issue_split()
            if (p, w) in up_at:
                k = up_at[(p, w)]
                split_up(k, fr("pt") if k > 5 else fr(("k", 0)) if k == 5 else [("t_q", Q.count["t_q"])])
                if k < 7:
                    load_up(k + 1)
            if p == 64 and w == 3:
                raw_ag = ag_raw[:, :].rearrange("p (k m) -> p k m", k=8)
                th = copy_hi(ag[:, :, 0, :], raw_ag, tok_ag, "a_ag")
                tok_ag = [th, sub_lo(PO, ag[:, :, 1, :], raw_ag, ag[:, :, 0, :], [th], "p_ag")]
            if p == 64 and w == 0:
                trans3(0)
            if p == 65 and w == 1:
                trans3(1)
            if w:
                wo_part(p, w)
            if p == 64 and w == 1:
                norm3(1)
            if p == 65 and w in (1, 3):
                gate(w // 2)
            if w < 2:
                if p < 64:
                    scores(p, w + 2)
                if w == 1 and p == 63:
                    for i in range(3):
                        load_x3(i, [("v_max", Q.count["v_max"])])
                if w == 0:
                    wo_part(p, w)
                if w == 0 and p == 65:
                    for k in range(4):
                        main3(0, k, 0, 0)
            elif p + 1 < 64:
                scores(p + 1, w - 2)
            elif w == 2 and p == 65:
                for k in range(4, 8):
                    main3(0, k, 0, 0)
        if p + 1 < 64:
            normalise(p + 1, 0)
        if p + 2 < 64:
            q_end(p + 2, tq)
        before_three(p)

    for bk in (4, 5):
        free[("b", bk)] = fr("o_bank") + fr(("b", 5))

    def z_turn(i):
        sl = i % 2
        t = transpose(ps[:, 6, 0:128], zs[:, sl, :], identf[:, :], [tok_z[i]] + fr(("b", 6)), "t_z")
        free[("zs", sl)] = [t]
        w = fr(("zt", sl))
        th = copy_hi(zth[:, sl, :], ps[:, 6, 0:128], [t] + w, "a_z")
        tl = sub_lo(DV, ztl[:, sl, :], ps[:, 6, 0:128], zth[:, sl, :], [th] + w, "v_zl")
        free[("b", 6)] = [tl]
        tok_zt[i] = [th, tl]

    tok_out = []

    def end3(i, bks):
        sl = i % 2
        for nh in range(2):
            t = mm3(bank(bks[nh]), zth[:, sl, :], ztl[:, sl, :], lbh[:, nh * 512:nh * 512 + 512],
                    lbl[:, nh * 512:nh * 512 + 512], False, True, tok_zt[i] + tok_lb, "t_l3")
            t2 = tt(y[:, sl, nh * 512:nh * 512 + 512], bank(bks[nh]), x3[:, i % 3, nh * 512:nh * 512 + 512], ALU.add,
                    [t, t_x3[i]] + fr(("y", sl)), "v_y")
            free[("b", bks[nh])] = [t2]
            tok_out.append(dma(out[i, :, nh * 512:nh * 512 + 512], y[:, sl, nh * 512:nh * 512 + 512], [t2],
                               f"d_y{sl}{nh}"))
        free[("h4t", sl)] = free[("zt", sl)] = [t]
        free[("x3", i % 3)] = [t2]
        free[("y", sl)] = tok_out[-2:]

    for i in range(8):
        bks = [[0, 1], [4, 5]][i % 2]
        if 1 <= i < 7:
            norm3(i + 1)
        for k in range(8 if i else 0):
            main3(i, k, 0, bks[0])
        if 1 <= i < 7:
            trans3(i + 1)
        z_turn(i)
        for k in range(8):
            main3(i, k, 1, bks[1])
        if 1 <= i < 7:
            gate(i + 1)
        end3(i, bks)
        if i + 3 < 8:
            load_x3(i + 3)
    Q.op(SP, lambda e: None, tok_out)

    block = ctx.enter_context(nc.Block())

    @block.sync
    def _(e):
        Q.emit(SP, e)

    @block.tensor
    def _(e):
        Q.emit(PE, e)

    @block.vector
    def _(e):
        Q.emit(DV, e)

    @block.scalar
    def _(e):
        Q.emit(AC, e)

    @block.gpsimd
    def _(e):
        Q.emit(PO, e)


def kernel(**inp):
    import ml_dtypes
    import numpy as np
    import concourse.bacc as bacc
    from concourse.bass_utils import run_bass_kernel_spmd as run

    def c(a):
        return np.ascontiguousarray(a)

    f = {k: np.asarray(v) for k, v in inp.items()}
    ctx = f["ctx_4096"]

    def slices(w, n):
        return c(w.reshape(8, 128, n, 128).transpose(2, 1, 0, 3).reshape(n, 128, 1024))

    def rows(w, m):
        return c(w.reshape(8, 128, m).transpose(1, 0, 2).reshape(128, 8 * m))

    inv = (np.float32(1.0) / (np.float64(10000.0) ** (np.arange(0, 128, 2, dtype=np.float32) / np.float32(128)))
           .astype(np.float32)).astype(np.float32)
    ang = (np.arange(1024, dtype=np.float32)[None, :] * inv[:, None]).astype(np.float32)
    cos, sin = np.cos(ang.astype(np.float64)), np.sin(ang.astype(np.float64))
    root = float(np.sqrt(np.float32(128.0)))
    cosk = np.concatenate([cos, cos], 0).astype(np.float32)
    sink = np.concatenate([sin, -sin], 0).astype(np.float32)
    cosq = (np.concatenate([cos, cos], 0)[:, :512] / root).astype(np.float32)
    sinq = (np.concatenate([sin, -sin], 0)[:, :512] / root).astype(np.float32)
    scal = np.concatenate([f[n].reshape(1) for n in
                           ("L0_xattn_x1_scale", "L0_xattn_x1_zp", "L0_xattn_x2_scale", "L0_xattn_x2_zp")])
    onehot = np.zeros((128, 8), np.float32)
    onehot[np.arange(128), np.arange(128) // 16] = 1
    rb = np.concatenate([np.tile(f["L0_ffn_router_b"][None, :], (128, 1)), onehot], 1)
    eb = np.concatenate([np.tile(f["L1_ffn_expert_bias"][None, :], (128, 1)), np.ones((128, 4), np.float32)], 1)
    arrays = {
        "identf": np.eye(128, dtype=np.float32),
        "identb": np.eye(128).astype(ml_dtypes.bfloat16),
        "onesb": np.ones((128, 128), ml_dtypes.bfloat16),
        "x": f["x"].reshape(8, 128, 1024),
        "ctx": ctx.reshape(2, 8, 128, 1024),
        "ctxT": ctx.transpose(0, 2, 1).reshape(2, 8, 128, 1024),
        "mask": f["mask_BxSxS2_ff0"].reshape(8, 128, 1024),
        "scal": np.tile(scal[None, :], (128, 1)),
        "cosk": cosk, "sink": sink, "cosq": cosq, "sinq": sinq,
        "wk": slices(f["L1_xattn_wk"], 8), "wv": slices(f["L1_xattn_wv"], 8), "wq": slices(f["L1_xattn_wq"], 32),
        "wo": f["L1_xattn_wo"].reshape(32, 128, 1024),
        "W": f["L0_ffn_W"].T.reshape(8, 128, 1024),
        "bias": np.tile(f["L0_ffn_b"][None, :], (128, 1)),
        "loraA": rows(f["L0_ffn_A"].reshape(128, 1024).T, 128),
        "loraB": f["L0_ffn_B"].transpose(0, 2, 1).reshape(128, 1024),
        "rw": rows(f["L0_ffn_router_W"].T, 8),
        "rb": rb, "eb": eb,
        "up": f["L1_ffn_W_up"].T.reshape(8, 128, 1024),
        "ag": rows(np.concatenate([f["L1_ffn_lora_A"].reshape(32, 1024).T, f["L1_ffn_gate_w"].T], 1), 36),
        "lb": f["L1_ffn_lora_B"].transpose(0, 2, 1).reshape(32, 1024),
    }
    nc = bacc.Bacc("TRN2", target_bir_lowering=False, num_devices=1)
    arrays = {"in_" + k: c(v) for k, v in arrays.items()}
    aps = {k[3:]: nc.dram_tensor(k, v.shape, mybir.dt.from_np(v.dtype), kind="ExternalInput").ap()
           for k, v in arrays.items()}
    o = nc.dram_tensor("out_0", (8, 128, 1024), F32, kind="ExternalOutput").ap()
    build(nc, aps, o)
    r = run(nc, [arrays], core_ids=[0])
    return r.results[0]["out_0"].reshape(2, 512, 1024)
```
